# Optimizing a Trainium2 kernel written in Bass

```python
import numpy as np
import jax
import jax.numpy as jnp

def _softmax(x, axis=-1):
    return jax.nn.softmax(x, axis=axis)

def _gelu(x):
    return jax.nn.gelu(x, approximate=True)

def _silu(x):
    return jax.nn.silu(x)

def _sigmoid(x):
    return jax.nn.sigmoid(x)

def _layernorm(x, axis=-1, eps=1e-05):
    m = jnp.mean(x, axis=axis, keepdims=True)
    v = jnp.var(x, axis=axis, keepdims=True)
    return (x - m) / jnp.sqrt(v + eps)

def _scatter_add(tgt, idx, src, axis=0):
    return tgt.at[idx].add(src)

def _segment_sum(src, seg, n):
    return jax.ops.segment_sum(src, seg, n)
kernel_name = 'mk_adaln_d1_jaxref_r8_e8f9ed'

def setup_inputs(seed: int=0):
    np.random.seed(seed)
    _w = jnp.asarray

    def _L0_attn_setup():
        import jax, jax.numpy as jnp
        import numpy as np
        import math
        B, S, DIM, HEADS = (2, 256, 128, 16)

        def _alibi_slopes(n_heads):

            def pow2_slopes(n):
                start = 2 ** (-2 ** (-(math.log2(n) - 3)))
                return [start * start ** i for i in range(n)]
            if math.log2(n_heads).is_integer():
                slopes = pow2_slopes(n_heads)
            else:
                closest = 2 ** math.floor(math.log2(n_heads))
                slopes = pow2_slopes(closest)
                slopes += pow2_slopes(2 * closest)[0::2][:n_heads - closest]
            return np.asarray(slopes, dtype=np.float32).reshape(n_heads, 1, 1)
        key = jax.random.key(seed)
        k1, k2, k3 = jax.random.split(key, 3)
        x = jax.random.normal(k1, (B, S, DIM), dtype=jnp.float32)
        W_qkv = jax.random.normal(k2, (3 * DIM, DIM), dtype=jnp.float32) * 0.02
        W_o = jax.random.normal(k3, (DIM, DIM), dtype=jnp.float32) * 0.02
        return {'x': x, 'W_qkv': W_qkv, 'W_o': W_o}
    _L0_attn_in = _L0_attn_setup()

    def _L0_ffn_setup():
        import jax, jax.numpy as jnp
        import numpy as np
        NUM_EXPERTS = 8
        HIDDEN = 128
        D_FF = 512
        SCALE = 0.8
        SPARSITY = 0.1

        def _perturb_attractive(w, scale=SCALE, sparsity=SPARSITY):
            a = jnp.abs(w)
            flat = a.ravel()
            n = flat.shape[0]
            k = max(1, int(n * sparsity / 2))
            s = jnp.sort(flat)
            thr_bot = s[k - 1]
            thr_top = s[n - k]
            tier = jnp.where(a >= thr_top, -1.0, jnp.where(a <= thr_bot, 1.0, 0.0))
            return w + scale * w * tier

        def _stack_expert_params(w):
            pw = _perturb_attractive(w)
            return jnp.concatenate([w[None], jnp.broadcast_to(pw, (NUM_EXPERTS - 1,) + w.shape)], axis=0)
        key = jax.random.key(seed)
        ks = jax.random.split(key, 6)
        B, S, H, F, E = (2, 256, HIDDEN, D_FF, NUM_EXPERTS)
        return {'x': jax.random.normal(ks[0], (B, S, H), dtype=jnp.float32), 'W1': jax.random.normal(ks[1], (H, F), dtype=jnp.float32) * (1.0 / np.sqrt(H)), 'b1': jax.random.normal(ks[2], (F,), dtype=jnp.float32) * 0.02, 'W2': jax.random.normal(ks[3], (F, H), dtype=jnp.float32) * (1.0 / np.sqrt(F)), 'b2': jax.random.normal(ks[4], (H,), dtype=jnp.float32) * 0.02, 'ln_gamma': jnp.ones((H,), dtype=jnp.float32), 'ln_beta': jnp.zeros((H,), dtype=jnp.float32), 'Wr': jax.random.normal(ks[5], (H, E), dtype=jnp.float32) * (1.0 / np.sqrt(H)), 'br': jnp.zeros((E,), dtype=jnp.float32)}
    _L0_ffn_in = _L0_ffn_setup()
    _L0_c = _w((lambda *s: np.random.randn(*s).astype(np.float32) * 0.05)(8, 128))
    _L0_wmod = _w((lambda *s: np.random.randn(*s).astype(np.float32) * 0.05)(128, 6 * 128) * 128 ** (-0.5))
    _d = {'L0_attn_x': _L0_attn_in['x'], 'L0_attn_W_qkv': _L0_attn_in['W_qkv'], 'L0_attn_W_o': _L0_attn_in['W_o'], 'L0_ffn_W1': _L0_ffn_in['W1'], 'L0_ffn_b1': _L0_ffn_in['b1'], 'L0_ffn_W2': _L0_ffn_in['W2'], 'L0_ffn_b2': _L0_ffn_in['b2'], 'L0_ffn_ln_gamma': _L0_ffn_in['ln_gamma'], 'L0_ffn_ln_beta': _L0_ffn_in['ln_beta'], 'L0_ffn_Wr': _L0_ffn_in['Wr'], 'L0_ffn_br': _L0_ffn_in['br'], 'L0_c': _L0_c, 'L0_wmod': _L0_wmod}
    _x0 = _d['L0_attn_x']
    _d['L0_attn_x'] = jax.random.normal(jax.random.fold_in(jax.random.key(seed), 1), (8, 256, 128), dtype=_x0.dtype)
    del _x0
    return _d

def reference(L0_attn_x, L0_attn_W_qkv, L0_attn_W_o, L0_ffn_W1, L0_ffn_b1, L0_ffn_W2, L0_ffn_b2, L0_ffn_ln_gamma, L0_ffn_ln_beta, L0_ffn_Wr, L0_ffn_br, L0_c, L0_wmod):

    def _L0_attn_ref(x, W_qkv, W_o):
        import jax, jax.numpy as jnp
        import numpy as np
        import math
        B, S, DIM, HEADS = (2, 256, 128, 16)

        def _alibi_slopes(n_heads):

            def pow2_slopes(n):
                start = 2 ** (-2 ** (-(math.log2(n) - 3)))
                return [start * start ** i for i in range(n)]
            if math.log2(n_heads).is_integer():
                slopes = pow2_slopes(n_heads)
            else:
                closest = 2 ** math.floor(math.log2(n_heads))
                slopes = pow2_slopes(closest)
                slopes += pow2_slopes(2 * closest)[0::2][:n_heads - closest]
            return np.asarray(slopes, dtype=np.float32).reshape(n_heads, 1, 1)
        b, s, d = x.shape
        h = HEADS
        hd = d // h
        scale = hd ** (-0.5)
        qkv = x @ W_qkv.T
        q, k, v = jnp.split(qkv, 3, axis=-1)
        q = q.reshape(b, s, h, hd).transpose(0, 2, 1, 3)
        k = k.reshape(b, s, h, hd).transpose(0, 2, 1, 3)
        v = v.reshape(b, s, h, hd).transpose(0, 2, 1, 3)
        scores = jnp.einsum('bhqd,bhkd->bhqk', q, k) * scale
        pos = jnp.arange(s)
        rel = (pos[None, :] - pos[:, None]).astype(scores.dtype)
        slopes = jnp.asarray(_alibi_slopes(h))
        scores = scores - slopes * rel
        causal_mask = pos[None, :] > pos[:, None]
        scores = jnp.where(causal_mask, jnp.finfo(scores.dtype).min, scores)
        weights = jax.nn.softmax(scores, axis=-1)
        out = jnp.einsum('bhqk,bhkd->bhqd', weights, v)
        out = out.transpose(0, 2, 1, 3).reshape(b, s, d)
        return out @ W_o.T

    def _L0_ffn_ref(x, W1, b1, W2, b2, ln_gamma, ln_beta, Wr, br):
        import jax, jax.numpy as jnp
        import numpy as np
        NUM_EXPERTS = 8
        HIDDEN = 128
        D_FF = 512
        SCALE = 0.8
        SPARSITY = 0.1

        def _perturb_attractive(w, scale=SCALE, sparsity=SPARSITY):
            a = jnp.abs(w)
            flat = a.ravel()
            n = flat.shape[0]
            k = max(1, int(n * sparsity / 2))
            s = jnp.sort(flat)
            thr_bot = s[k - 1]
            thr_top = s[n - k]
            tier = jnp.where(a >= thr_top, -1.0, jnp.where(a <= thr_bot, 1.0, 0.0))
            return w + scale * w * tier

        def _stack_expert_params(w):
            pw = _perturb_attractive(w)
            return jnp.concatenate([w[None], jnp.broadcast_to(pw, (NUM_EXPERTS - 1,) + w.shape)], axis=0)
        mu = jnp.mean(x, axis=-1, keepdims=True)
        var = jnp.mean(jnp.square(x - mu), axis=-1, keepdims=True)
        h = (x - mu) * jax.lax.rsqrt(var + 1e-05) * ln_gamma + ln_beta
        logits = jnp.einsum('bsh,he->bse', h, Wr) + br
        probs = jax.nn.softmax(logits, axis=-1)
        W1s = _stack_expert_params(W1)
        b1s = _stack_expert_params(b1)
        W2s = _stack_expert_params(W2)
        b2s = _stack_expert_params(b2)
        pre = jnp.einsum('bsh,ehf->besf', x, W1s) + b1s[None, :, None, :]
        act = jax.nn.gelu(pre)
        y = jnp.einsum('besf,efh->besh', act, W2s) + b2s[None, :, None, :]
        out = jnp.einsum('bse,besh->bsh', probs, y)
        return out
    x = L0_attn_x
    mod = (_silu(L0_c) @ L0_wmod).reshape(L0_c.shape[0], 6, 1, -1)
    sa, ca, ga, sb, cb, gb = (mod[:, 0], mod[:, 1], mod[:, 2], mod[:, 3], mod[:, 4], mod[:, 5])
    ga = (2 * (ga >= 0) - 1) * jnp.maximum(jnp.abs(ga), 0.25)
    gb = (2 * (gb >= 0) - 1) * jnp.maximum(jnp.abs(gb), 0.25)
    h = _layernorm(x, axis=-1) * (1 + ca) + sa
    x = x + ga * _L0_attn_ref(h, L0_attn_W_qkv, L0_attn_W_o)
    h = _layernorm(x, axis=-1) * (1 + cb) + sb
    x = x + gb * _L0_ffn_ref(h, L0_ffn_W1, L0_ffn_b1, L0_ffn_W2, L0_ffn_b2, L0_ffn_ln_gamma, L0_ffn_ln_beta, L0_ffn_Wr, L0_ffn_br)
    return x

_drawn_inputs = setup_inputs


def setup_inputs(seed=0):
    import zlib

    import numpy as np

    out = dict(_drawn_inputs(seed))
    spreads = {'L0_ffn_ln_gamma': (1.0, 0.6), 'L0_ffn_ln_beta': (0.0, 2.0), 'L0_ffn_br': (0.0, 2.0)}
    factors = {'L0_attn_W_qkv': 8.0,
     'L0_attn_W_o': 8.0,
     'L0_ffn_b1': 26.916,
     'L0_ffn_b2': 8.0,
     'L0_ffn_Wr': 3.939}
    for name, (base, spread) in spreads.items():
        noise = np.random.default_rng([zlib.crc32(name.encode()), seed]).standard_normal(out[name].shape)
        drawn = base * np.exp(spread * noise) if base else spread * noise
        out[name] = jnp.asarray(drawn.astype(out[name].dtype))
    for name, factor in factors.items():
        out[name] = (out[name] * factor).astype(out[name].dtype)
    return out
```

```python
from contextlib import ExitStack
import math

import numpy as np

import concourse.bass as bass
from concourse import mybir

F32 = mybir.dt.float32
BF16 = mybir.dt.bfloat16
U32 = mybir.dt.uint32
ALU = mybir.AluOpType
ACT = mybir.ActivationFunctionType
AX = mybir.AxisListType

P = 128
B, S, D = 8, 256, 128
NH, HD = 16, 8
NBLK = S // P
FF = 512
NC = FF // P
NE = 8
G = 4
HG = NH // G
NPART = 3
R_PROD = NPART * NPART * HD
R_BIAS = 6
R_MAX = 2
R_S = R_PROD + R_BIAS
R_E = R_S + R_MAX
M_LAG, E_LAG = 5, 10
SEL0 = 5
NBITS = 31
NEG = -1.0e30
EPS = 1e-5
ROTS = 3
K_STAT = int(P * FF * 0.1 / 2)
K_B1 = int(FF * 0.1 / 2)
K_B2 = int(D * 0.1 / 2)
LAST_E = B * G + E_LAG
T_END = LAST_E + 4
C0_STEP = M_LAG + B * G + 1
NPAIR = B // 2
POOL_SETS = 12


def adaln_block(nc, x, w_qkv, w_o, w1, b1, w2, b2, gamma, beta, wr, br, c, wmod,
                k_const, q_const, ident_c, mask_c, parts_dram, out):
    with ExitStack() as ctx:
        def sb(name, shape, dt=F32):
            return ctx.enter_context(nc.sbuf_tensor(name, shape, dt))

        def sem(name):
            return ctx.enter_context(nc.semaphore(name))

        x_all = sb("x_all", [P, B, NBLK, D])
        ident = sb("ident", [P, P])
        mask4 = sb("mask4", [P, HG, P], BF16)
        identb = sb("identb", [P, P], BF16)
        ones_b = sb("ones_b", [P, P], BF16)
        wqkv_in = sb("wqkv_in", [P, 3, D])
        wo_in = sb("wo_in", [P, D])
        wqkT = sb("wqkT", [P, 2, D])
        wvT = sb("wvT", [P, D])
        woT = sb("woT", [P, D])
        woTg = sb("woTg", [P, B, D])
        w1_sb = sb("w1_sb", [P, FF])
        w2_sb = sb("w2_sb", [P, NC, D])
        w1p = sb("w1p", [P, FF])
        w2p = sb("w2p", [P, NC, D])
        w1a = sb("w1a", [P, FF])
        w2a = sb("w2a", [P, FF])
        b1_bc = sb("b1_bc", [P, FF])
        b2_bc = sb("b2_bc", [P, D])
        b2p_bc = sb("b2p_bc", [P, D])
        br_bc = sb("br_bc", [P, NE])
        vecs = sb("vecs", [NC + 3, P])
        cols = sb("cols", [P, NC + 3])
        colsa = sb("colsa", [P, NC + 3])
        b1p = sb("b1p", [P, NC])
        wr_sb = sb("wr_sb", [P, NE])
        wrg = sb("wrg", [P, NE])
        beta_w = sb("beta_w", [P, P])
        gsum = sb("gsum", [P, 2 * NE])
        c_in = sb("c_in", [B, D])
        c_t = sb("c_t", [P, B])
        c_e = sb("c_e", [P, B])
        c_s = sb("c_s", [P, B])
        wmod_sb = sb("wmod_sb", [P, 6 * D])
        modT = sb("modT", [P, 2, B])
        rows = sb("rows", [B, 4, D])
        rowt = sb("rowt", [B, 2, D])
        onehot = sb("onehot", [B, B, P])
        rows_bc = sb("rows_bc", [P, B, 4, D])
        st1 = sb("st1", [P, B * NBLK, 6])
        mv1 = sb("mv1", [P, B * NBLK, 2])
        ve1 = sb("ve1", [P, B * NBLK])
        rs1 = sb("rs1", [P, B * NBLK])
        mhalf = sb("mhalf", [P, B * NBLK])
        n1 = sb("n1", [P, 2, NBLK, D])
        h1T = sb("h1T", [P, 2, S])
        part8 = sb("part8", [P, 2, 6, S], BF16)
        resid = sb("resid", [P, 2, S])
        Qs = sb("Qs", [R_E, ROTS, NH, S], BF16)
        Ks = sb("Ks", [R_E, ROTS, NH, S], BF16)
        Vx = sb("Vx", [P, 4, NBLK, NH, 32])
        nmax = sb("nmax", [P, 2, NBLK, NH])
        nmT = sb("nmT", [NH, 2, R_MAX, S], BF16)
        PT = sb("PT", [P, 2, 3, HG * P])
        U = sb("U", [P, 2, S])
        rden = sb("rden", [P, NBLK, HG])
        A = sb("A", [P, 2, NBLK, D])
        AT = sb("AT", [P, S])
        msk = sb("msk", [P, 4, FF], BF16)
        cnt = sb("cnt", [P, 4, NC], BF16)
        ktab = sb("ktab", [P, 4])
        cond = sb("cond", [P, 4], U32)
        cur = sb("cur", [P, 4], U32)
        cand = sb("cand", [P, 4], U32)

        n2 = sb("n2", [P, 2, 4, D])
        h2 = sb("h2", [P, 2, 4, D])
        h2T = sb("h2T", [P, 2, 4 * P])
        mv3 = sb("mv3", [P, B * NBLK, 2])
        ve3 = sb("ve3", [P, B * NBLK])
        rs3 = sb("rs3", [P, B * NBLK])
        lgT = sb("lgT", [NE, 4 * P])
        lg = sb("lg", [P, 4, NE])
        lt = sb("lt", [P, 4, NE])
        ex = sb("ex", [P, 4, NE])
        eul = sb("eul", [P, 4, NE])
        lmax = sb("lmax", [P, 4])
        esum = sb("esum", [P, 4])
        esum1 = sb("esum1", [P, 4])
        pr = sb("pr", [P, 2, 2, 4])
        hid = sb("hid", [P, 2, NC, 4 * P])
        yt = sb("yt", [P, 2, 4, D])
        ob = sb("ob", [P, 2, 4, D])
        b1a = sb("b1a", [P, FF])
        b2a = sb("b2a", [P, D])
        b2t = sb("b2t", [P, D])
        rank = sb("rank", [P, 2, NC])
        rtmp = sb("rtmp", [P, NC])

        banks = [ctx.enter_context(nc.psum_tensor(f"bank{i}", [P, 512], F32)) for i in range(8)]
        psS, psE, psO, psU, psQ, psX = banks[0:2], banks[2:4], banks[4], banks[5], banks[6], banks[7]

        x_in = [sem(f"x_in{b}") for b in range(B)]
        names = ["qkvw_in", "small_in", "w1_in", "w2_in", "const_in", "bc_in",
                 "pool_set", "dve_set", "act_set", "pe_set",
                 "ln_stat", "ln_rstd", "n1_done", "t_done", "h1_done", "qk_done", "v_done", "v_out",
                 "hi_done", "res_done", "split_done", "s_done", "max_done", "nmT_done", "nmhi_done",
                 "nmlo_done", "e_done", "exp_done", "sel_done", "pv_done", "u_done", "ut_done",
                 "rd_done", "a_done", "at_done", "at_out", "y_done", "x2_done", "rb_done", "rb_out",
                 "wog_done", "cand_done", "m_dve", "m_act", "m_pool", "cnt_done", "cnt_out",
                 "tot_done", "ln2_stat", "ln2_rstd", "n2_done", "h2m", "h2_done", "ln3_stat", "ln3_rstd",
                 "h2T_psum", "h2T_done", "lgT_done", "lgT_out", "lg_psum", "lg_read", "logit_done", "ex_done",
                 "f1_done", "f2_done", "gelu_done", "y_read", "ob_done", "pert_done", "b1p_done",
                 "b2m_done", "b2rank", "b2p_done", "dve_self", "pool_self", "act_self"]
        q = {n: sem(n) for n in names}
        part_w = [sem(f"part_w{i}") for i in range(2)]
        stack_in = [sem(f"stack_in{i}") for i in range(ROTS)]
        stored = [sem(f"stored{i}") for i in range(2)]
        mrow_in = [sem(f"mrow_in{i}") for i in range(2)]

        psF = (psS[0], psS[1], psE[0])
        block = ctx.enter_context(nc.Block())
        ROT = lambda b: b % ROTS

        def p_step(t):
            return (t // G, t % G) if t // G < B else (None, None)

        def lagged(t, lag):
            k = t - lag
            return (k // G, k % G, k) if 0 <= k < B * G else (None, None, None)

        def sel_bit(t):
            n = t - SEL0
            return n if 0 <= n < NBITS else None

        SETS = {}
        count = 0
        for name, k in (("onehot", 1), ("sil1", 1), ("sil2", 1), ("silu", 1), ("wq", 1), ("wk", 1), ("wv", 1),
                        ("wo", 1), ("cols", 1), ("wrg", 1), ("beta", 1), ("sa", 1), ("modT", 1),
                        ("absg", 1), ("maxg", 1), ("sgn", 1), ("sgn2", 1), ("gates", 1), ("cb", 1), ("rows", 1), ("gs", 1), ("all", 1)):
            count += k
            SETS[name] = count

        @block.sync
        def _(sp):
            sp.dma_start(x_all[:, 0], x[0].rearrange("(i p) d -> p i d", p=P)).then_inc(x_in[0], 16)
            sp.dma_start(c_in[:, :], c).then_inc(q["small_in"], 16)
            sp.dma_start(ident[:, :], ident_c).then_inc(q["small_in"], 16)
            sp.dma_start(vecs[0:NC, :], b1.rearrange("(c p) -> c p", p=P)).then_inc(q["small_in"], 16)
            for r, v in enumerate((b2, gamma, beta)):
                sp.dma_start(vecs[NC + r:NC + r + 1, :], v.rearrange("(a n) -> a n", a=1)).then_inc(q["small_in"], 16)
            sp.dma_start(wmod_sb[:, :], wmod).then_inc(q["small_in"], 16)
            sp.dma_start(wr_sb[:, :], wr).then_inc(q["small_in"], 16)
            for b in range(1, B):
                sp.dma_start(x_all[:, b], x[b].rearrange("(i p) d -> p i d", p=P)).then_inc(x_in[b], 16)
            sp.dma_start(w1_sb[:, :], w1).then_inc(q["w1_in"], 16)
            sp.dma_start(w2_sb[:, :, :], w2.rearrange("(c p) d -> p c d", p=P)).then_inc(q["w2_in"], 16)
            sp.dma_start(b1_bc[:, :], b1.partition_broadcast(P)).then_inc(q["bc_in"], 16)
            sp.dma_start(b2_bc[:, :], b2.partition_broadcast(P)).then_inc(q["bc_in"], 16)
            sp.dma_start(br_bc[:, :], br.partition_broadcast(P)).then_inc(q["bc_in"], 16)

            def stack(b):
                i = b % 2
                sp.wait_ge(q["split_done"], b + 1)
                sp.dma_start(parts_dram[b, 0:6].rearrange("s p t -> p s t"), part8[:, i]).then_inc(part_w[i], 16)
                sp.dma_start(parts_dram[b, 6:8].rearrange("s p t -> p s t"), part8[:, i, 3:5]).then_inc(part_w[i], 16)
                if b >= ROTS:
                    sp.wait_ge(q["e_done"], 3 * G * (b - ROTS + 1))
                sp.wait_ge(part_w[i], 32 * (b // 2 + 1))
                rowsz = NPART * HD
                for r in range(3):
                    sp.dma_start(Qs[rowsz * r:rowsz * (r + 1), ROT(b)],
                                 parts_dram[b, 0:3].rearrange("s (d h) t -> (s d) h t", d=HD)).then_inc(stack_in[ROT(b)], 16)
                    sp.dma_start(Ks[rowsz * r:rowsz * (r + 1), ROT(b)],
                                 parts_dram[b, 3 + r:6 + r].rearrange("s (d h) t -> (s d) h t", d=HD)).then_inc(stack_in[ROT(b)], 16)

            def mrows(b):
                sp.wait_ge(q["nmlo_done"], b + 1)
                sp.dma_start(Qs[R_S:R_S + 1, ROT(b)], nmT[:, b % 2, 0, :]).then_inc(mrow_in[b % 2], 16)
                sp.dma_start(Qs[R_S + 1:R_E, ROT(b)], nmT[:, b % 2, 1, :]).then_inc(mrow_in[b % 2], 16)

            for t in range(T_END):
                b, g = p_step(t)
                if b is not None and g == 2:
                    stack(b)
                bl, gl, _ = lagged(t, M_LAG + 4)
                if bl is not None and gl == 0:
                    mrows(bl)
            for p in range(NPAIR):
                sp.wait_ge(q["ob_done"], p + 1)
                sp.dma_start(out[2 * p:2 * p + 2].rearrange("b (i t) d -> t (b i) d", t=P), ob[:, p % 2]).then_inc(stored[p % 2], 16)
            for s in stored:
                sp.wait_ge(s, 16 * NPAIR // 2)

        @block.gpsimd
        def _(gp):
            gp.memset(ones_b[:, :], 1.0).then_inc(q["pool_set"], 1)
            gp.memset(mhalf[:, :], -0.5).then_inc(q["pool_set"], 1)
            for i in range(4):
                gp.memset(Vx[:, i], 1.0).then_inc(q["pool_set"], 1)
            gp.memset(beta_w[:, :], 1.0).then_inc(q["pool_set"], 1)
            for col, k in enumerate((K_STAT - 1, P * FF - K_STAT,
                                     2 * (P * FF - K_STAT) - P * FF, 2 * (K_STAT - 1) - P * FF)):
                gp.memset(ktab[:, col:col + 1], float(k)).then_inc(q["pool_set"], 1)

            def rstd(n0, n1_, k):
                gp.wait_ge(q["ln_stat"], k)
                gp.tensor_scalar(ve1[:, n0:n1_], mv1[:, n0:n1_, 1], EPS, None, op0=ALU.add).then_inc(q["pool_self"], 1)
                gp.wait_ge(q["pool_self"], k)
                gp.tensor_tensor(rs1[:, n0:n1_], ve1[:, n0:n1_], mhalf[:, n0:n1_], op=ALU.pow).then_inc(q["ln_rstd"], 1)

            def c_pool(p):
                own = B + 2 * p
                ks = slice(4 * p, 4 * p + 4)
                gp.wait_ge(q["ln2_stat"], p + 1)
                gp.tensor_scalar(ve1[:, ks], mv1[:, ks, 1], EPS, None, op0=ALU.add).then_inc(q["pool_self"], 1)
                gp.wait_ge(q["pool_self"], own + 1)
                gp.tensor_tensor(rs1[:, ks], ve1[:, ks], mhalf[:, ks], op=ALU.pow).then_inc(q["ln2_rstd"], 1)
                gp.wait_ge(q["n2_done"], p + 1)
                gp.wait_ge(q["rb_out"], B)
                if p >= 2:
                    gp.wait_ge(q["h2T_psum"], p - 1)
                for k in range(2):
                    bc = [rows_bc[:, 2 * p + k, r, :].unsqueeze(1).broadcast_to([P, NBLK, D]) for r in (2, 3)]
                    hv = h2[:, p % 2, 2 * k:2 * k + 2, :]
                    gp.tensor_tensor(hv, n2[:, p % 2, 2 * k:2 * k + 2, :], bc[0], op=ALU.mult).then_inc(q["h2m"], 1)
                    gp.wait_ge(q["h2m"], 2 * p + k + 1)
                    gp.tensor_tensor(hv, hv, bc[1], op=ALU.add).then_inc(q["h2_done"], 1)
                gp.wait_ge(q["ln3_stat"], p + 1)
                gp.tensor_scalar(ve3[:, ks], mv3[:, ks, 1], EPS, None, op0=ALU.add).then_inc(q["pool_self"], 1)
                gp.wait_ge(q["pool_self"], own + 2)
                gp.tensor_tensor(rs3[:, ks], ve3[:, ks], mhalf[:, ks], op=ALU.pow).then_inc(q["ln3_rstd"], 1)

            def c_exp(p):
                gp.wait_ge(q["logit_done"], p + 1)
                gp.tensor_tensor(ex[:, :, :], eul[:, :, :], lg[:, :, :], op=ALU.pow).then_inc(q["ex_done"], 1)

            gp.memset(eul[:, :, :], math.e).then_inc(q["pool_set"], 1)
            gp.wait_ge(q["pool_set"], POOL_SETS)
            rstd(0, NBLK, 1)
            for t in range(T_END):
                b, g = p_step(t)
                if b is not None and g == 1 and b + 1 < B:
                    rstd(NBLK * (b + 1), NBLK * (b + 2), b + 2)
                if sel_bit(t) is not None:
                    n = sel_bit(t)
                    gp.wait_ge(q["cand_done"], n + 1)
                    if n:
                        gp.wait_ge(q["cnt_done"], n)
                    gp.tensor_scalar(msk[:, 1], w2a[:, :], cand[:, 1:2].bitcast(F32), None, op0=ALU.is_lt).then_inc(q["m_pool"], 1)
                b, g, e = lagged(t, E_LAG)
                if b is not None:
                    for j in range(3):
                        gp.wait_ge(q["exp_done"], 3 * e + j + 1)
                        if j == 0:
                            v = PT[:, e % 2, 0].rearrange("p (h q) -> p h q", h=HG)
                        else:
                            v = PT[:, e % 2, j].rearrange("p (h q) -> p h q", h=2)[:, :, 0:P]
                        gp.affine_select(out=v, in_=v, compare_op=ALU.is_ge, fill=0.0, base=0,
                                         pattern=[[0, v.shape[1]], [1, P]], channel_multiplier=-1).then_inc(q["sel_done"], 1)
                if t == C0_STEP:
                    c_pool(0)
            c_exp(0)
            for p in range(1, NPAIR):
                c_pool(p)
                c_exp(p)

        @block.scalar
        def _(act):
            act.dma_start(wqkv_in[:, :, :], w_qkv.rearrange("(j p) d -> p j d", p=P)).then_inc(q["qkvw_in"], 16)
            act.dma_start(wo_in[:, :], w_o).then_inc(q["qkvw_in"], 16)
            act.dma_start(identb[:, :], mask_c[:, 4 * P:5 * P]).then_inc(q["const_in"], 16)
            act.dma_start(mask4[:, :, :], mask_c[:, 0:4 * P].rearrange("p (h k) -> p h k", h=HG)).then_inc(q["const_in"], 16)
            for r in range(ROTS):
                act.dma_start(Qs[R_PROD:R_S, r], q_const.rearrange("r (h t) -> r h t", h=NH)).then_inc(q["const_in"], 16)
                act.dma_start(Ks[R_PROD:R_E, r], k_const.rearrange("r (h t) -> r h t", h=NH)).then_inc(q["const_in"], 16)
            act.wait_ge(q["pe_set"], 1)
            act.activation(c_e[:, :], psQ[:, 0:B], ACT.Exp, scale=-1.0).then_inc(q["act_set"], 1)
            act.wait_ge(q["w1_in"], 16)
            act.activation(w1a[:, :], w1_sb[:, :], ACT.Abs).then_inc(q["act_set"], 1)
            act.wait_ge(q["w2_in"], 16)
            act.activation(w2a[:, :], w2_sb.rearrange("p c d -> p (c d)"), ACT.Abs).then_inc(q["act_set"], 1)

            def p_act(b, g):
                if g == 0:
                    act.wait_ge(q["t_done"], b + 1)
                    if b >= 2:
                        act.wait_ge(q["v_done"], b - 1)
                    if b == 0:
                        act.wait_ge(q["dve_set"], SETS["modT"])
                    act.activation(h1T[:, b % 2], psQ[:, 0:S], ACT.Identity, scale=modT[:, 1, b:b + 1],
                                   bias=modT[:, 0, b:b + 1]).then_inc(q["h1_done"], 1)
                if g == 1:
                    act.wait_ge(q["qk_done"], b + 1)
                    if b >= 2:
                        act.wait_ge(part_w[b % 2], 32 * (b // 2))
                    act.activation(part8[:, b % 2, 0:4:3, :], psQ.rearrange("p (a t) -> p a t", a=2),
                                   ACT.Copy).then_inc(q["hi_done"], 1)
                    act.wait_ge(q["v_done"], b + 1)
                    if b == 0:
                        act.wait_ge(q["pool_set"], POOL_SETS)
                    if b >= 4:
                        act.wait_ge(q["pv_done"], G * (b - 3))
                    act.activation(Vx[:, b % 4, :, :, 0:HD],
                                   psX[:, 0:S].rearrange("p (i h d) -> p i h d", i=NBLK, h=NH),
                                   ACT.Copy).then_inc(q["v_out"], 1)
                if g == 2:
                    act.wait_ge(q["rb_done"], b + 1)
                    act.activation(rows_bc[:, b], psX[:, :].rearrange("p (r d) -> p r d", r=4), ACT.Copy).then_inc(q["rb_out"], 1)

            for t in range(T_END):
                n = sel_bit(t)
                if n is not None:
                    act.wait_ge(q["cand_done"], n + 1)
                    if n:
                        act.wait_ge(q["cnt_done"], n)
                    for col, w in ((2, w1a), (3, w2a)):
                        act.activation(msk[:, col], w[:, :], ACT.Sign, bias=cand[:, col:col + 1].bitcast(F32),
                                       scale=-(1.0 - 2.0 ** -24)).then_inc(q["m_act"], 1)
                b, g, e = lagged(t, E_LAG)
                if b is not None:
                    for j in range(3):
                        u = 3 * e + j
                        act.wait_ge(q["e_done"], u + 1)
                        if e >= 2 and j == 0:
                            act.wait_ge(q["pv_done"], e - 1)
                        act.activation(PT[:, e % 2, j], psE[u % 2][:, :], ACT.Exp).then_inc(q["exp_done"], 1)
                bm, gm, _ = lagged(t, M_LAG + 4)
                if bm is not None and gm == 0:
                    act.wait_ge(q["nmT_done"], bm + 1)
                    if bm >= 2:
                        act.wait_ge(mrow_in[bm % 2], 32 * (bm // 2))
                    act.activation(nmT[:, bm % 2, 0, :], psX[0:NH, 0:S], ACT.Copy).then_inc(q["nmhi_done"], 1)
                b, g, e = lagged(t, E_LAG + 1)
                if b is not None:
                    act.wait_ge(q["pv_done"], e + 1)
                    if e >= 2:
                        act.wait_ge(q["ut_done"], e - 1)
                    act.activation(U[:, e % 2], psO[:, 0:S], ACT.Copy).then_inc(q["u_done"], 1)
                b, g, e = lagged(t, E_LAG + 3)
                b, g, _ = lagged(t, E_LAG + 2)
                if b is not None and g == 3:
                    act.wait_ge(q["at_done"], b + 1)
                    if b:
                        act.wait_ge(q["y_done"], b)
                    act.activation(AT[:, :], psX[:, 0:S], ACT.Copy).then_inc(q["at_out"], 1)
                b, g = p_step(t)
                if b is not None:
                    p_act(b, g)
            def c_act_h(p):
                act.wait_ge(q["h2T_psum"], p + 1)
                if p >= 2:
                    act.wait_ge(q["f1_done"], 4 * 2 * (p - 1))
                    act.wait_ge(q["lgT_done"], p - 1)
                act.activation(h2T[:, p % 2], psE[1][:, :], ACT.Copy).then_inc(q["h2T_done"], 1)

            def c_act_l(p):
                act.wait_ge(q["lgT_done"], p + 1)
                if p:
                    act.wait_ge(q["lg_psum"], p)
                act.activation(lgT[:, :], psQ[0:NE, :], ACT.Copy).then_inc(q["lgT_out"], 1)

            c_act_h(0)
            c_act_l(0)
            for n in range(2 * NPAIR):
                p, w = n // 2, n % 2
                for ch in range(NC):
                    act.wait_ge(q["f1_done"], 4 * n + ch + 1)
                    if n >= 2 and ch == 0:
                        act.wait_ge(q["f2_done"], n - 1)
                    if n == 1 and ch == 0:
                        act.wait_ge(q["b1p_done"], 1)
                    bias = b1p[:, ch:ch + 1] if w else cols[:, ch:ch + 1]
                    act.activation(hid[:, n % 2, ch, :], psF[(4 * n + ch) % 3][:, :], ACT.Gelu_apprx_tanh,
                                   bias=bias).then_inc(q["gelu_done"], 1)
                if w and p + 1 < NPAIR:
                    c_act_h(p + 1)
                    c_act_l(p + 1)

        @block.tensor
        def _(pe):
            mm = nc.tensor.matmul
            tr = nc.tensor.transpose
            pe.wait_ge(q["small_in"], 16 * 8)
            tr(psQ[:, 0:B], c_in[:, :], ident[0:B, 0:B]).then_inc(q["pe_set"], 1)
            pe.wait_ge(q["qkvw_in"], 32)
            for j in range(3):
                tr(psS[0][:, j * P:(j + 1) * P], wqkv_in[:, j, :], ident[:, :])
            tr(psS[0][:, 3 * P:4 * P], wo_in[:, :], ident[:, :]).then_inc(q["pe_set"], 1)
            tr(psS[1][:, 0:NC + 3], vecs[:, :], ident[0:NC + 3, 0:NC + 3]).then_inc(q["pe_set"], 1)
            pe.wait_ge(q["dve_set"], SETS["silu"])
            for j in range(2):
                mm(psE[0][:, j * B:(j + 1) * B], wmod_sb[:, j * D:(j + 1) * D], c_s[:, :], start=True, stop=True)
            mm(psE[1][0:B, 0:512], c_s[:, :], wmod_sb[:, 2 * D:6 * D], start=True, stop=True).then_inc(q["pe_set"], 1)
            pe.wait_ge(q["pool_set"], POOL_SETS)
            pe.wait_ge(q["dve_set"], SETS["wrg"])
            mm(psO[:, 0:NE], beta_w[:, :], wrg[:, :], start=True, stop=True)
            pe.wait_ge(q["dve_set"], SETS["beta"])
            mm(psO[:, NE:2 * NE], woTg[:, 0, :], wr_sb[:, :], start=True, stop=True).then_inc(q["pe_set"], 1)

            def s_unit(t, j):
                b, g, m = lagged(t, M_LAG)
                if b is None:
                    return
                u, r, bank = 3 * m + j, ROT(b), psS[(3 * m + j) % 2]
                if m == 0 and j == 0:
                    pe.wait_ge(q["const_in"], 16 * (2 + 2 * ROTS))
                    pe.wait_ge(q["dve_set"], SETS["all"])
                if g == 0 and j == 0:
                    pe.wait_ge(stack_in[r], 96 * (b // ROTS + 1))
                if u >= 2:
                    pe.wait_ge(q["max_done"], u - 1)
                if j == 0:
                    mm(bank[:, :], identb[:, :], mask4.rearrange("p h k -> p (h k)"), start=True, stop=False, skip_group_check=True)
                    for i in range(HG):
                        h = HG * g + i
                        last = mm(bank[:, i * P:(i + 1) * P], Qs[0:R_S, r, h, 0:P], Ks[0:R_S, r, h, 0:P],
                                  start=False, stop=True, skip_group_check=True)
                else:
                    mm(bank.rearrange("p (h k) -> p h k", h=2)[:, :, P:S], identb[:, :], mask4[:, 0:2, :],
                       start=True, stop=False, skip_group_check=True)
                    for i in range(2):
                        h = HG * g + 2 * (j - 1) + i
                        last = mm(bank[:, i * S:(i + 1) * S], Qs[0:R_S, r, h, P:S], Ks[0:R_S, r, h, :],
                                  start=False, stop=True, skip_group_check=True)
                last.then_inc(q["s_done"], 1)

            def e_unit(t, j):
                b, g, e = lagged(t, E_LAG)
                if b is None:
                    return
                u, r, bank = 3 * e + j, ROT(b), psE[(3 * e + j) % 2]
                if g == 0 and j == 0:
                    pe.wait_ge(mrow_in[b % 2], 32 * (b // 2 + 1))
                if u >= 2:
                    pe.wait_ge(q["exp_done"], u - 1)
                if j == 0:
                    for i in range(HG):
                        h = HG * g + i
                        last = mm(bank[:, i * P:(i + 1) * P], Ks[0:R_E, r, h, P:S], Qs[0:R_E, r, h, P:S],
                                  start=True, stop=True, skip_group_check=True)
                else:
                    for i in range(2):
                        h = HG * g + 2 * (j - 1) + i
                        last = mm(bank[:, i * S:(i + 1) * S], Ks[0:R_E, r, h, 0:P], Qs[0:R_E, r, h, :],
                                  start=True, stop=True, skip_group_check=True)
                last.then_inc(q["e_done"], 1)

            def pv(t):
                b, g, e = lagged(t, E_LAG + 1)
                if b is None:
                    return
                pe.wait_ge(q["sel_done"], 3 * e + 3)
                if g == 0:
                    pe.wait_ge(q["v_out"], b + 1)
                if e:
                    pe.wait_ge(q["u_done"], e)
                pt0 = PT[:, e % 2, 0].rearrange("p (h q) -> p h q", h=HG)
                for i in range(HG):
                    h = HG * g + i
                    mm(psO[32 * i:32 * i + 32, 0:S], Vx[:, b % 4, 0, h, :],
                       PT[:, e % 2, 1 + i // 2, (i % 2) * S:(i % 2 + 1) * S], start=True, stop=False,
                       skip_group_check=True)
                for i in range(HG):
                    h = HG * g + i
                    last = mm(psO[32 * i:32 * i + 32, P:S], Vx[:, b % 4, 1, h, :], pt0[:, i, :],
                              start=False, stop=True, skip_group_check=True)
                last.then_inc(q["pv_done"], 1)

            def ut(t):
                b, g, e = lagged(t, E_LAG + 2)
                if b is None:
                    return
                pe.wait_ge(q["u_done"], e + 1)
                if e:
                    pe.wait_ge(q["a_done"], e)
                for i in range(NBLK):
                    last = tr(psU[:, i * P:(i + 1) * P], U[:, e % 2, i * P:(i + 1) * P], ident[:, :])
                last.then_inc(q["ut_done"], 1)

            free_x = [None]

            def claim_x(reader):
                if free_x[0]:
                    pe.wait_ge(*free_x[0])
                free_x[0] = reader

            for t in range(T_END):
                for j in range(3):
                    s_unit(t, j)
                bm, gm, _ = lagged(t, M_LAG + 4)
                if bm is not None and gm == 0:
                    pe.wait_ge(q["max_done"], 3 * G * (bm + 1))
                    claim_x((q["nmlo_done"], bm + 1))
                    for i in range(NBLK):
                        last = tr(psX[0:NH, i * P:(i + 1) * P], nmax[:, bm % 2, i, :], ident[:, :])
                    last.then_inc(q["nmT_done"], 1)
                ut(t)
                e_unit(t, 0)
                e_unit(t, 1)
                n = sel_bit(t)
                e_unit(t, 2)
                if n is not None:
                    pe.wait_ge(q["m_dve"], n + 1)
                    pe.wait_ge(q["m_act"], 2 * n + 2)
                    pe.wait_ge(q["m_pool"], n + 1)
                    claim_x((q["cnt_out"], n + 1))
                    for col in range(4):
                        for ch in range(NC):
                            last = mm(psX[:, col * NC + ch:col * NC + ch + 1], msk[:, col, ch * P:(ch + 1) * P],
                                      ones_b[:, 0:1], start=True, stop=True, skip_group_check=True)
                    last.then_inc(q["cnt_done"], 1)
                pv(t)
                if n is not None:
                    claim_x((q["cand_done"], n + 2))
                    for ch in range(NC):
                        last = mm(psX[:, 0:4], ones_b[:, :], cnt[:, :, ch], start=(ch == 0), stop=(ch == NC - 1))
                    last.then_inc(q["tot_done"], 1)
                b, g, _ = lagged(t, E_LAG + 2)
                if b is not None and g == 3:
                    pe.wait_ge(q["a_done"], G * (b + 1))
                    claim_x((q["at_out"], b + 1))
                    for i in range(NBLK):
                        last = tr(psX[:, i * P:(i + 1) * P], A[:, b % 2, i, :], ident[:, :])
                    last.then_inc(q["at_done"], 1)
                    pe.wait_ge(q["wog_done"], b + 1)
                    claim_x((q["x2_done"], b + 1))
                    for i in range(NBLK):
                        last = mm(psX[:, i * P:(i + 1) * P], AT[:, i * P:(i + 1) * P], woTg[:, b, :], start=True, stop=True)
                    last.then_inc(q["y_done"], 1)
                b, g = p_step(t)
                if b is not None and g == 0:
                    pe.wait_ge(q["n1_done"], b + 1)
                    if b == 0:
                        pe.wait_ge(q["act_set"], 1)
                    else:
                        pe.wait_ge(q["res_done"], b)
                    for i in range(NBLK):
                        last = tr(psQ[:, i * P:(i + 1) * P], n1[:, b % 2, i, :], ident[:, :])
                    last.then_inc(q["t_done"], 1)
                if b is not None and g == 1:
                    pe.wait_ge(q["h1_done"], b + 1)
                    for a in range(2):
                        last = mm(psQ[:, a * S:(a + 1) * S], wqkT[:, a, :], h1T[:, b % 2], start=True, stop=True)
                    last.then_inc(q["qk_done"], 1)
                    claim_x((q["v_out"], b + 1))
                    for i in range(NBLK):
                        last = mm(psX[:, i * P:(i + 1) * P], h1T[:, b % 2, i * P:(i + 1) * P], wvT[:, :], start=True, stop=True)
                    last.then_inc(q["v_done"], 1)
                if b is not None and g == 2:
                    claim_x((q["rb_out"], b + 1))
                    mm(psX[:, :], onehot[:, b, :], rows.rearrange("b r d -> b (r d)"), start=True, stop=True).then_inc(q["rb_done"], 1)
            def c_pe_h(p):
                pe.wait_ge(q["h2_done"], 2 * p + 2)
                if p:
                    pe.wait_ge(q["h2T_done"], p)
                for i in range(4):
                    last = tr(psE[1][:, i * P:(i + 1) * P], h2[:, p % 2, i, :], ident[:, :])
                last.then_inc(q["h2T_psum"], 1)

            def c_pe_l(p):
                pe.wait_ge(q["h2T_done"], p + 1)
                if p:
                    pe.wait_ge(q["lgT_out"], p)
                mm(psQ[0:NE, :], wrg[:, :], h2T[:, p % 2], start=True, stop=True).then_inc(q["lgT_done"], 1)

            def c_pe_t(p):
                pe.wait_ge(q["lgT_out"], p + 1)
                claim_x((q["lg_read"], p + 1))
                for i in range(4):
                    last = tr(psX[:, i * NE:(i + 1) * NE], lgT[:, i * P:(i + 1) * P], ident[0:NE, 0:NE])
                last.then_inc(q["lg_psum"], 1)

            def f1(n):
                p, w = n // 2, n % 2
                wt = w1p if w else w1_sb
                if w == 0:
                    pe.wait_ge(q["h2T_done"], p + 1)
                if n == 1:
                    pe.wait_ge(q["pert_done"], 1)
                for ch in range(NC):
                    k = 4 * n + ch
                    if k == 0:
                        pe.wait_ge(q["max_done"], 3 * G * B)
                        pe.wait_ge(q["exp_done"], 3 * G * B)
                    if k >= 3:
                        pe.wait_ge(q["gelu_done"], k - 2)
                    mm(psF[k % 3][:, :], wt[:, ch * P:(ch + 1) * P], h2T[:, p % 2], start=True, stop=True).then_inc(q["f1_done"], 1)

            def f2(n):
                p, w = n // 2, n % 2
                wt, bank = (w2p, psU) if w else (w2_sb, psO)
                if p:
                    pe.wait_ge(q["y_read"], n - 1)
                if n == 1:
                    pe.wait_ge(q["pert_done"], 2)
                pe.wait_ge(q["gelu_done"], 4 * (n + 1))
                for i in range(4):
                    for ch in range(NC):
                        last = mm(bank[:, i * P:(i + 1) * P], hid[:, n % 2, ch, i * P:(i + 1) * P], wt[:, ch, :],
                                  start=(ch == 0), stop=(ch == NC - 1), skip_group_check=True)
                last.then_inc(q["f2_done"], 1)

            pe.wait_ge(q["b2m_done"], 1)
            claim_x((q["b2p_done"], 1))
            mm(psX[:, 0:2 * P], ones_b[:, :], msk[:, 2, 0:2 * P], start=True, stop=True).then_inc(q["b2rank"], 1)
            pe.wait_ge(q["exp_done"], 3 * G * B)
            pe.wait_ge(q["a_done"], G * B)
            c_pe_h(0)
            c_pe_l(0)
            for n in range(2 * NPAIR + 1):
                if n < 2 * NPAIR:
                    f1(n)
                if n % 2 == 0 and n // 2 < NPAIR:
                    c_pe_t(n // 2)
                if n % 2 and (n + 1) // 2 < NPAIR:
                    c_pe_h((n + 1) // 2)
                if n:
                    f2(n - 1)
                if n % 2 and (n + 1) // 2 < NPAIR:
                    c_pe_l((n + 1) // 2)

        @block.vector
        def _(v):
            ve = nc.vector
            own = [0]

            def then_self(inst):
                own[0] += 1
                inst.then_inc(q["dve_self"], 1)
                v.wait_ge(q["dve_self"], own[0])

            def absolute(dst, src):
                return ve.tensor_scalar(dst.bitcast(U32), src.bitcast(U32), 0x7FFFFFFF, None, op0=ALU.bitwise_and)

            def ln1(b):
                v.wait_ge(x_in[b], 16)
                for i in range(NBLK):
                    last = ve.bn_stats(st1[:, 2 * b + i, :], x_all[:, b, i, :])
                then_self(last)
                for i in range(NBLK):
                    last = ve.bn_aggr(mv1[:, 2 * b + i, :], st1[:, 2 * b + i, :])
                last.then_inc(q["ln_stat"], 1)

            ln1(0)
            v.wait_ge(q["small_in"], 16 * 8)
            ds = lambda inst: inst.then_inc(q["dve_set"], 1)
            ds(ve.tensor_copy(onehot[:, :, :], ident[0:B, 0:B].unsqueeze(2).broadcast_to([B, B, P])))
            v.wait_ge(q["act_set"], 1)
            ds(ve.tensor_scalar(c_e[:, :], c_e[:, :], 1.0, None, op0=ALU.add))
            v.wait_ge(q["dve_set"], SETS["sil1"])
            ds(ve.reciprocal(c_e[:, :], c_e[:, :]))
            v.wait_ge(q["dve_set"], SETS["sil2"])
            ds(ve.tensor_tensor(c_s[:, :], psQ[:, 0:B], c_e[:, :], op=ALU.mult))
            v.wait_ge(q["pe_set"], 2)
            ds(ve.tensor_scalar(wqkT[:, 0, :].rearrange("p (d h) -> p h d", d=HD),
                                psS[0][:, 0:P].rearrange("p (h d) -> p h d", h=NH), float(HD) ** -0.5, None, op0=ALU.mult))
            ds(ve.tensor_copy(wqkT[:, 1, :].rearrange("p (d h) -> p h d", d=HD),
                              psS[0][:, P:2 * P].rearrange("p (h d) -> p h d", h=NH)))
            ds(ve.tensor_copy(wvT[:, :], psS[0][:, 2 * P:3 * P]))
            ds(ve.tensor_copy(woT[:, :], psS[0][:, 3 * P:4 * P]))
            v.wait_ge(q["pe_set"], 3)
            ds(ve.tensor_copy(cols[:, :], psS[1][:, 0:NC + 3]))
            v.wait_ge(q["dve_set"], SETS["cols"])
            ds(ve.tensor_scalar(wrg[:, :], wr_sb[:, :], cols[:, NC + 1:NC + 2], None, op0=ALU.mult))
            ds(ve.tensor_copy(woTg[:, 0, :], cols[:, NC + 2:NC + 3].broadcast_to([P, P])))
            v.wait_ge(q["pe_set"], 4)
            ds(ve.tensor_copy(modT[:, 0, :], psE[0][:, 0:B]))
            ds(ve.tensor_scalar(modT[:, 1, :], psE[0][:, B:2 * B], 1.0, None, op0=ALU.add))
            pg = psE[1][0:B, :].rearrange("b (r d) -> b r d", r=4)
            ds(absolute(rows[:, 0:2, :], pg[:, 0:4:3, :]))
            v.wait_ge(q["dve_set"], SETS["absg"])
            ds(ve.tensor_scalar(rows[:, 0:2, :], rows[:, 0:2, :], 0.25, None, op0=ALU.max))
            ds(ve.tensor_scalar(rowt[:, :, :], pg[:, 0:4:3, :], 0.0, 2.0, op0=ALU.is_ge, op1=ALU.mult))
            v.wait_ge(q["dve_set"], SETS["sgn"])
            ds(ve.tensor_scalar(rowt[:, :, :], rowt[:, :, :], -1.0, None, op0=ALU.add))
            v.wait_ge(q["dve_set"], SETS["sgn2"])
            ds(ve.tensor_tensor(rows[:, 0:2, :], rows[:, 0:2, :], rowt[:, :, :], op=ALU.mult))
            ds(ve.tensor_scalar(rows[:, 2, :], pg[:, 2, :], 1.0, None, op0=ALU.add))
            ds(ve.tensor_copy(rows[:, 3, :], pg[:, 1, :]))
            v.wait_ge(q["pe_set"], 5)
            v.wait_ge(q["bc_in"], 48)
            ds(ve.tensor_copy(gsum[:, 0:NE], psO[:, 0:NE]))
            ds(ve.tensor_tensor(gsum[:, NE:2 * NE], psO[:, NE:2 * NE], br_bc[:, :], op=ALU.add))
            v.wait_ge(q["pool_set"], POOL_SETS)

            def first_cand():
                top = 1 << (NBITS - 1)
                then_self(ve.memset(cur[:, :], 0))
                v.wait_ge(q["act_set"], 3)
                ve.tensor_scalar(cand[:, 0:2], cur[:, 0:2], top, None, op0=ALU.bitwise_or)
                ve.tensor_scalar(cand[:, 2:4], cur[:, 2:4], top - 1, None, op0=ALU.bitwise_or).then_inc(q["cand_done"], 1)

            def update(n):
                bit = NBITS - 1 - n
                v.wait_ge(q["tot_done"], n + 1)
                then_self(ve.tensor_tensor(cond[:, :], psX[:, 0:4], ktab[:, :], op=ALU.is_le))
                if bit:
                    then_self(ve.tensor_scalar(cond[:, :], cond[:, :], bit, None, op0=ALU.logical_shift_left))
                then_self(ve.tensor_tensor(cur[:, :], cur[:, :], cond[:, :], op=ALU.bitwise_or))
                nxt = 1 << (bit - 1) if bit else 0
                ve.tensor_scalar(cand[:, 0:2], cur[:, 0:2], nxt, None, op0=ALU.bitwise_or)
                ve.tensor_scalar(cand[:, 2:4], cur[:, 2:4], max(nxt - 1, 0), None, op0=ALU.bitwise_or).then_inc(q["cand_done"], 1)

            def maxima(t, j):
                b, g, m = lagged(t, M_LAG)
                if b is None:
                    return
                if g == 0 and j == 0 and b >= 2:
                    v.wait_ge(q["nmT_done"], b - 1)
                v.wait_ge(q["s_done"], 3 * m + j + 1)
                bank = psS[(3 * m + j) % 2]
                if j == 0:
                    ve.tensor_reduce(nmax[:, b % 2, 0, HG * g:HG * (g + 1)], bank.rearrange("p (h k) -> p h k", h=HG),
                                     axis=AX.X, op=ALU.max, negate=True).then_inc(q["max_done"], 1)
                else:
                    h = HG * g + 2 * (j - 1)
                    ve.tensor_reduce(nmax[:, b % 2, 1, h:h + 2], bank.rearrange("p (h k) -> p h k", h=2),
                                     axis=AX.X, op=ALU.max, negate=True).then_inc(q["max_done"], 1)

            def c_ln(p):
                xp = x_all[:, 2 * p:2 * p + 2].rearrange("p b i d -> p (b i) d")
                v.wait_ge(q["x2_done"], 2 * p + 2)
                for i in range(4):
                    last = ve.bn_stats(st1[:, 4 * p + i, :], xp[:, i, :])
                then_self(last)
                for i in range(4):
                    last = ve.bn_aggr(mv1[:, 4 * p + i, :], st1[:, 4 * p + i, :])
                last.then_inc(q["ln2_stat"], 1)
                v.wait_ge(q["ln2_rstd"], p + 1)
                if p >= 2:
                    v.wait_ge(q["h2_done"], 2 * p - 2)
                for i in range(4):
                    k = 4 * p + i
                    last = ve.tensor_scalar(n2[:, p % 2, i, :], xp[:, i, :], mv1[:, k, 0:1], rs1[:, k:k + 1],
                                            op0=ALU.subtract, op1=ALU.mult)
                last.then_inc(q["n2_done"], 1)
                v.wait_ge(q["h2_done"], 2 * p + 2)
                for i in range(4):
                    last = ve.bn_stats(st1[:, 4 * p + i, :], h2[:, p % 2, i, :])
                then_self(last)
                for i in range(4):
                    last = ve.bn_aggr(mv3[:, 4 * p + i, :], st1[:, 4 * p + i, :])
                last.then_inc(q["ln3_stat"], 1)

            def router(p):
                ks = slice(4 * p, 4 * p + 4)
                e8 = lambda a: a.unsqueeze(2).broadcast_to([P, 4, NE])
                g8 = lambda a: a.unsqueeze(1).broadcast_to([P, 4, NE])
                v.wait_ge(q["ln3_stat"], p + 1)
                then_self(ve.tensor_tensor(lt[:, :, :], e8(mv3[:, ks, 0]), g8(gsum[:, 0:NE]), op=ALU.mult))
                v.wait_ge(q["lg_psum"], p + 1)
                ve.tensor_tensor(lg[:, :, :], psX[:, 0:4 * NE].rearrange("p (i e) -> p i e", i=4), lt[:, :, :],
                                 op=ALU.subtract).then_inc(q["lg_read"], 1)
                v.wait_ge(q["lg_read"], p + 1)
                v.wait_ge(q["ln3_rstd"], p + 1)
                then_self(ve.tensor_tensor(lg[:, :, :], lg[:, :, :], e8(rs3[:, ks]), op=ALU.mult))
                then_self(ve.tensor_tensor(lg[:, :, :], lg[:, :, :], g8(gsum[:, NE:2 * NE]), op=ALU.add))
                then_self(ve.tensor_reduce(lmax[:, :], lg[:, :, :], axis=AX.X, op=ALU.max))
                ve.tensor_tensor(lg[:, :, :], lg[:, :, :], e8(lmax[:, :]), op=ALU.subtract).then_inc(q["logit_done"], 1)
                v.wait_ge(q["ex_done"], p + 1)
                ve.tensor_reduce(esum[:, :], ex[:, :, :], axis=AX.X, op=ALU.add)
                then_self(ve.tensor_reduce(esum1[:, :], ex[:, :, 1:NE], axis=AX.X, op=ALU.add))
                then_self(ve.reciprocal(esum[:, :], esum[:, :]))
                ve.tensor_tensor(pr[:, p % 2, 0, :], ex[:, :, 0], esum[:, :], op=ALU.mult)
                then_self(ve.tensor_tensor(pr[:, p % 2, 1, :], esum1[:, :], esum[:, :], op=ALU.mult))

            def combine(n):
                p, w = n // 2, n % 2
                bias = (b2p_bc if w else b2_bc)[:, :].unsqueeze(1).broadcast_to([P, 4, D])
                bank = (psU if w else psO).rearrange("p (i d) -> p i d", i=4)
                v.wait_ge(q["f2_done"], n + 1)
                if w == 0 and p >= 2:
                    v.wait_ge(stored[p % 2], 16 * (p // 2))
                dst = yt[:, w]
                ve.tensor_tensor(dst, bank, bias, op=ALU.add).then_inc(q["y_read"], 1)
                v.wait_ge(q["y_read"], n + 1)
                then_self(ve.tensor_tensor(dst, dst, pr[:, p % 2, w, :].unsqueeze(2).broadcast_to([P, 4, D]), op=ALU.mult))
                if w:
                    then_self(ve.tensor_tensor(yt[:, 1], yt[:, 1], yt[:, 0], op=ALU.add))
                    for k in range(2):
                        bs = slice(2 * k, 2 * k + 2)
                        last = ve.tensor_tensor(yt[:, 1, bs], yt[:, 1, bs],
                                                rows_bc[:, 2 * p + k, 1, :].unsqueeze(1).broadcast_to([P, NBLK, D]), op=ALU.mult)
                    then_self(last)
                    ve.tensor_tensor(ob[:, p % 2], yt[:, 1], x_all[:, 2 * p:2 * p + 2].rearrange("p b i d -> p (b i) d"),
                                     op=ALU.add).then_inc(q["ob_done"], 1)

            def perturb(w, a, top, bot, dst):
                t0, t1 = msk[:, 0], msk[:, 1]
                then_self(ve.tensor_scalar(t0, a, top.bitcast(F32), None, op0=ALU.is_ge))
                then_self(ve.scalar_tensor_tensor(t1, a, bot.bitcast(F32), t0, op0=ALU.is_le, op1=ALU.is_gt))
                then_self(ve.tensor_tensor(t1, t1, t0, op=ALU.subtract))
                then_self(ve.scalar_tensor_tensor(dst, w, 0.8, t1, op0=ALU.mult, op1=ALU.mult))
                ve.tensor_tensor(dst, dst, w, op=ALU.add).then_inc(q["pert_done"], 1)

            def tiers(low, high, w, dst, tmp, k, done):
                then_self(ve.tensor_scalar(tmp, high, float(k - 1), None, op0=ALU.is_le))
                then_self(ve.scalar_tensor_tensor(dst, low, float(k - 1), tmp, op0=ALU.is_le, op1=ALU.is_gt))
                then_self(ve.tensor_tensor(dst, dst, tmp, op=ALU.subtract))
                then_self(ve.scalar_tensor_tensor(dst, w, 0.8, dst, op0=ALU.mult, op1=ALU.mult))
                ve.tensor_tensor(dst, dst, w, op=ALU.add).then_inc(q[done], 1)

            def perturb_b1():
                then_self(absolute(colsa[:, :], cols[:, :]))
                then_self(absolute(b1a[:, :], b1_bc[:, :]))
                for ch in range(NC):
                    for k, op in enumerate((ALU.is_lt, ALU.is_gt)):
                        last = ve.tensor_scalar(msk[:, k], b1a[:, :], colsa[:, ch:ch + 1], None, op0=op, op1=ALU.add,
                                                accum_out=rank[:, k, ch:ch + 1])
                    then_self(last)
                tiers(rank[:, 0, :], rank[:, 1, :], cols[:, 0:NC], b1p[:, :], rtmp[:, :], K_B1, "b1p_done")
                then_self(absolute(b2a[:, :], b2_bc[:, :]))
                ve.tensor_scalar(msk[:, 2, 0:P], b2a[:, :], colsa[:, NC:NC + 1], None, op0=ALU.is_gt)
                ve.tensor_scalar(msk[:, 2, P:2 * P], b2a[:, :], colsa[:, NC:NC + 1], None, op0=ALU.is_lt).then_inc(q["b2m_done"], 1)

            def perturb_b2():
                v.wait_ge(q["b2rank"], 1)
                tiers(psX[:, 0:P], psX[:, P:2 * P], b2_bc[:, :], b2p_bc[:, :], b2t[:, :], K_B2, "b2p_done")

            for t in range(T_END):
                n = sel_bit(t)
                if t == SEL0:
                    first_cand()
                if n is not None:
                    if n:
                        v.wait_ge(q["cnt_done"], n)
                    v.wait_ge(q["cand_done"], n + 1)
                    ve.tensor_scalar(msk[:, 0], w1a[:, :], cand[:, 0:1].bitcast(F32), None, op0=ALU.is_lt).then_inc(q["m_dve"], 1)
                for j in range(3):
                    maxima(t, j)
                b, g, e = lagged(t, E_LAG + 2)
                if b is not None:
                    v.wait_ge(q["ut_done"], e + 1)
                    pu = psU[:, 0:S].rearrange("p (i h r) -> p i h r", i=NBLK, h=HG)
                    then_self(ve.reciprocal(rden[:, :, :], pu[:, :, :, HD]))
                    if g == 0 and b >= 2:
                        v.wait_ge(q["at_done"], b - 1)
                    ve.tensor_tensor(A[:, b % 2, :, HG * HD * g:HG * HD * (g + 1)].rearrange("p i (h d) -> p i h d", h=HG),
                                     pu[:, :, :, 0:HD], rden[:, :, :].unsqueeze(3).broadcast_to([P, NBLK, HG, HD]),
                                     op=ALU.mult).then_inc(q["a_done"], 1)
                bm, gm, _ = lagged(t, M_LAG + 4)
                if bm is not None and gm == 0:
                    v.wait_ge(q["nmhi_done"], bm + 1)
                    ve.tensor_tensor(nmT[:, bm % 2, 1, :], psX[0:NH, 0:S], nmT[:, bm % 2, 0, :], op=ALU.subtract).then_inc(q["nmlo_done"], 1)
                if n is not None:
                    v.wait_ge(q["cnt_done"], n + 1)
                    ve.tensor_copy(cnt.rearrange("p a c -> p (a c)"), psX[:, 0:4 * NC]).then_inc(q["cnt_out"], 1)
                    update(n)
                b, g, _ = lagged(t, E_LAG + 2)
                if b is not None and g == 3:
                    v.wait_ge(q["y_done"], b + 1)
                    ve.tensor_tensor(x_all[:, b], x_all[:, b], psX[:, 0:S].rearrange("p (i d) -> p i d", i=NBLK),
                                     op=ALU.add).then_inc(q["x2_done"], 1)
                b, g = p_step(t)
                if b is not None and g == 0:
                    v.wait_ge(q["ln_rstd"], b + 1)
                    if b >= 2:
                        v.wait_ge(q["t_done"], b - 1)
                    for i in range(NBLK):
                        k = 2 * b + i
                        last = ve.tensor_scalar(n1[:, b % 2, i, :], x_all[:, b, i, :], mv1[:, k, 0:1], rs1[:, k:k + 1],
                                                op0=ALU.subtract, op1=ALU.mult)
                    last.then_inc(q["n1_done"], 1)
                    if b + 1 < B:
                        ln1(b + 1)
                if b is not None and g == 1:
                    i = b % 2
                    v.wait_ge(q["hi_done"], b + 1)
                    pq = psQ.rearrange("p (a t) -> p a t", a=2)
                    inst = ve.tensor_tensor(resid[:, :, :], pq, part8[:, i, 0:4:3, :], op=ALU.subtract)
                    inst.then_inc(q["res_done"], 1)
                    v.wait_ge(q["res_done"], b + 1)
                    then_self(ve.tensor_copy(part8[:, i, 1:5:3, :], resid[:, :, :]))
                    ve.tensor_tensor(part8[:, i, 2:6:3, :], resid[:, :, :], part8[:, i, 1:5:3, :], op=ALU.subtract).then_inc(q["split_done"], 1)
                if b is not None and g == 2:
                    v.wait_ge(q["rb_out"], b + 1)
                    if b == 0:
                        v.wait_ge(q["pe_set"], 5)
                    ve.tensor_tensor(woTg[:, b, :], woT[:, :], rows_bc[:, b, 0, :], op=ALU.mult).then_inc(q["wog_done"], 1)
                if t == C0_STEP:
                    c_ln(0)
                if t == C0_STEP + 1:
                    perturb(w1_sb[:, :], w1a[:, :], cur[:, 2:3], cur[:, 0:1], w1p[:, :])
                if t == C0_STEP + 2:
                    flat = lambda a: a.rearrange("p c d -> p (c d)")
                    perturb(flat(w2_sb), w2a[:, :], cur[:, 1:2], cur[:, 3:4], flat(w2p))
                if t == C0_STEP + 3:
                    perturb_b1()
            perturb_b2()
            router(0)
            for n in range(1, 2 * NPAIR + 1):
                if n % 2 and (n + 1) // 2 < NPAIR:
                    c_ln((n + 1) // 2)
                combine(n - 1)
                if n % 2 == 0 and n // 2 < NPAIR:
                    router(n // 2)


def slopes():
    start = 2 ** (-2 ** (-(math.log2(NH) - 3)))
    return np.asarray([start * start ** i for i in range(NH)], np.float32)


def bf16_bits(a):
    return (np.ascontiguousarray(a, np.float32).view(np.uint32) >> 16).astype(np.uint16)


def constants():
    rest = slopes()
    sp = []
    for _ in range(3):
        part = (rest.view(np.uint32) & 0xFFFF0000).view(np.float32)
        sp.append(part)
        rest = rest - part
    pos = np.arange(S, dtype=np.float32)
    kc = np.ones((R_BIAS + R_MAX, NH, S), np.float32)
    qc = np.zeros((R_BIAS, NH, S), np.float32)
    for i in range(3):
        kc[i] = sp[i][:, None]
        qc[i] = pos[None, :]
        kc[3 + i] = pos[None, :]
        qc[3 + i] = -sp[i][:, None]
    above = np.where(np.arange(P)[None, :] > np.arange(P)[:, None], NEG, 0.0)
    mask = np.concatenate([above] * HG + [np.eye(P)], axis=1)
    return {"k_const": bf16_bits(kc.reshape(-1, NH * S)), "q_const": bf16_bits(qc.reshape(-1, NH * S)),
            "ident_c": np.eye(P, dtype=np.float32), "mask_c": bf16_bits(mask)}


_INS = [("L0_attn_x", "x"), ("L0_attn_W_qkv", "w_qkv"), ("L0_attn_W_o", "w_o"), ("L0_ffn_W1", "w1"), ("L0_ffn_b1", "b1"),
        ("L0_ffn_W2", "w2"), ("L0_ffn_b2", "b2"), ("L0_ffn_ln_gamma", "gamma"), ("L0_ffn_ln_beta", "beta"),
        ("L0_ffn_Wr", "wr"), ("L0_ffn_br", "br"), ("L0_c", "c"), ("L0_wmod", "wmod")]


def kernel(**inputs):
    import concourse.bacc as bacc
    from concourse.bass_utils import run_bass_kernel_spmd

    nc = bacc.Bacc("TRN2", target_bir_lowering=False, num_devices=1)
    arrays = {f"in_{short}": np.ascontiguousarray(inputs[name]) for name, short in _INS}
    arrays.update({f"in_{name}": a for name, a in constants().items()})
    args = [nc.dram_tensor(n, a.shape, mybir.dt.from_np(a.dtype), kind="ExternalInput").ap() for n, a in arrays.items()]
    parts = nc.dram_tensor("parts", [B, 8, P, S], BF16, kind="Internal").ap()
    out = nc.dram_tensor("out_0", [B, S, D], F32, kind="ExternalOutput").ap()
    args = [a.bitcast(BF16) if a.dtype == mybir.dt.uint16 else a for a in args]
    adaln_block(nc, *args, parts, out)
    r = run_bass_kernel_spmd(nc, [arrays], core_ids=[0])
    return r.results[0]["out_0"]
```

```python
from contextlib import ExitStack
import math

import numpy as np

import concourse.bass as bass
from concourse import mybir

F32 = mybir.dt.float32
BF16 = mybir.dt.bfloat16
U32 = mybir.dt.uint32
ALU = mybir.AluOpType
ACT = mybir.ActivationFunctionType
AX = mybir.AxisListType

P = 128
B, S, D = 8, 256, 128
NH, HD = 16, 8
NBLK = S // P
FF = 512
NC = FF // P
NE = 8
G = 4
HG = NH // G
NPART = 3
R_PROD = NPART * NPART * HD
R_BIAS = 6
R_MAX = 2
R_S = R_PROD + R_BIAS
R_E = R_S + R_MAX
M_LAG, E_LAG = 7, 12
SEL0 = 4
AT_N1, AT_T, AT_QK, AT_SPLIT, AT_V = 0, 1, 2, 3, 4
AT_NMT = M_LAG + G
AT_OT, AT_Y = E_LAG + G + 1, E_LAG + G + 2
NBITS = 31
NEG = -1.0e30
EPS = 1e-5
ROTS = 3
K_STAT = int(P * FF * 0.1 / 2)
K_B1 = int(FF * 0.1 / 2)
K_B2 = int(D * 0.1 / 2)
ROWS_AT = {3 + i: (2 * i, 2 * i + 1) for i in range(B // 2)}
T_END = AT_Y + G * (B - 1) + 1
C_STEPS = {37: 0, 40: 1, 43: 2}
W1_STEP, W2_STEP, B1_STEP, B2_STEP = 36, 38, 41, 42
FFN_STEP = E_LAG + B * G
assert SEL0 + NBITS < W1_STEP and AT_Y + G * 5 < 43
NPAIR = B // 2
POOL_SETS = 12


def adaln_block(nc, x, w_qkv, w_o, w1, b1, w2, b2, gamma, beta, wr, br, c, wmod,
                k_const, q_const, ident_c, mask_c, parts_dram, out):
    with ExitStack() as ctx:
        def sb(name, shape, dt=F32):
            return ctx.enter_context(nc.sbuf_tensor(name, shape, dt))

        def sem(name):
            return ctx.enter_context(nc.semaphore(name))

        x_all = sb("x_all", [P, B, NBLK, D])
        ident = sb("ident", [P, P])
        mask5 = sb("mask5", [P, HG + 1, P], BF16)
        ones_b = sb("ones_b", [P, P], BF16)
        wqkv_in = sb("wqkv_in", [P, 3, D])
        wo_in = sb("wo_in", [P, D])
        wqkT = sb("wqkT", [P, 2, D])
        wvT = sb("wvT", [P, D])
        woT = sb("woT", [P, D])
        woTg = sb("woTg", [P, B, D])
        w1_sb = sb("w1_sb", [P, FF])
        w2_sb = sb("w2_sb", [P, NC, D])
        w1p = sb("w1p", [P, FF])
        w2p = sb("w2p", [P, NC, D])
        w1a = sb("w1a", [P, FF])
        w2a = sb("w2a", [P, FF])
        b1_bc = sb("b1_bc", [P, FF])
        b2_bc = sb("b2_bc", [P, D])
        b2p_bc = sb("b2p_bc", [P, D])
        br_bc = sb("br_bc", [P, NE])
        vecs = sb("vecs", [NC + 3, P])
        cols = sb("cols", [P, NC + 3])
        colsa = sb("colsa", [P, NC + 3])
        b1p = sb("b1p", [P, NC])
        wr_sb = sb("wr_sb", [P, NE])
        wrg = sb("wrg", [P, NE])
        beta_w = sb("beta_w", [P, P])
        gsum = sb("gsum", [P, 2 * NE])
        c_in = sb("c_in", [B, D])
        c_t = sb("c_t", [P, B])
        c_e = sb("c_e", [P, B])
        c_s = sb("c_s", [P, B])
        wmod_sb = sb("wmod_sb", [P, 6 * D])
        modT = sb("modT", [P, 2, B])
        rows = sb("rows", [B, 4, D])
        rowt = sb("rowt", [B, 2, D])
        onehot = sb("onehot", [B, B, P])
        rows_bc = sb("rows_bc", [P, B, 4, D])
        st1 = sb("st1", [P, B * NBLK, 6])
        mv1 = sb("mv1", [P, B * NBLK, 2])
        ve1 = sb("ve1", [P, B * NBLK])
        rs1 = sb("rs1", [P, B * NBLK])
        mhalf = sb("mhalf", [P, B * NBLK])
        n1 = sb("n1", [P, 2, NBLK, D])
        h1T = sb("h1T", [P, 2, S])
        part8 = sb("part8", [P, 2, 6, S], BF16)
        resid = sb("resid", [P, 2, S])
        Qs = sb("Qs", [R_E, ROTS, NH, S], BF16)
        Ks = sb("Ks", [R_E, ROTS, NH, S], BF16)
        Vx = sb("Vx", [P, 4, NBLK, NH, 32])
        nmax = sb("nmax", [P, 2, NBLK, NH])
        nmT = sb("nmT", [NH, 2, R_MAX, S], BF16)
        PT = sb("PT", [P, 2, 3, HG * P])
        U = sb("U", [P, 2, S])
        rden = sb("rden", [P, NBLK, HG])
        A = sb("A", [P, 2, NBLK, D])
        AT = sb("AT", [P, S])
        msk = sb("msk", [P, 4, FF], BF16)
        cnt = sb("cnt", [P, 4, NC], BF16)
        ktab = sb("ktab", [P, 4])
        cond = sb("cond", [P, 4], U32)
        cur = sb("cur", [P, 4], U32)
        cand = sb("cand", [P, 4], U32)
        nxt = sb("nxt", [P, 4], U32)

        n2 = sb("n2", [P, 4, D])
        h2 = sb("h2", [P, NPAIR, 4, D])
        h2T = sb("h2T", [P, 2, 4 * P])
        mv3 = sb("mv3", [P, B * NBLK, 2])
        ve3 = sb("ve3", [P, B * NBLK])
        rs3 = sb("rs3", [P, B * NBLK])
        lgT = sb("lgT", [NE, 4 * P])
        lg = sb("lg", [P, 4, NE])
        lt = sb("lt", [P, 4, NE])
        ex = sb("ex", [P, 4, NE])
        eul = sb("eul", [P, 4, NE])
        lmax = sb("lmax", [P, 4])
        esum = sb("esum", [P, 4])
        esum1 = sb("esum1", [P, 4])
        pr = sb("pr", [P, 2, 2, 4])
        hid = sb("hid", [P, 2, NC, 4 * P])
        yt = sb("yt", [P, 2, 4, D])
        ob = sb("ob", [P, 2, 4, D])
        b1a = sb("b1a", [P, FF])
        b2a = sb("b2a", [P, D])
        b2t = sb("b2t", [P, D])
        rank = sb("rank", [P, 2, NC])
        rtmp = sb("rtmp", [P, NC])

        banks = [ctx.enter_context(nc.psum_tensor(f"bank{i}", [P, 512], F32)) for i in range(8)]
        psS, psE, psO, psU, psQ, psX = banks[0:2], banks[2:4], banks[4], banks[5], banks[6], banks[7]

        x_in = [sem(f"x_in{b}") for b in range(B)]
        names = ["qkvw_in", "c_in", "ident_in", "wmod_in", "vec_in", "w1_in", "w2_in", "const_in", "bc_in",
                 "pool_set", "dve_set", "act_set", "pe_set",
                 "ln_stat", "ln_rstd", "n1_done", "t_done", "h1_done", "qk_done", "v_done", "v_out",
                 "hi_done", "res_done", "split_done", "s_done", "max_done", "nmT_done", "nmhi_done",
                 "nmlo_done", "e_done", "exp_done", "sel_done", "pv_done", "u_done", "ut_done",
                 "rd_done", "a_done", "at_done", "at_out", "y_done", "x2_done", "rb_done", "rb_out",
                 "wog_done", "cand_done", "m_dve", "m_act", "m_pool", "cnt_done", "cnt_out",
                 "tot_done", "cond_done", "ln2_stat", "ln2_rstd", "h2_done", "ln3_stat", "ln3_rstd",
                 "h2T_psum", "h2T_done", "lgT_done", "lgT_out", "lg_psum", "lg_read", "logit_done", "ex_done",
                 "f1_done", "f2_done", "gelu_done", "y_read", "ob_done", "pert_done", "b1p_done",
                 "b2m_done", "b2rank", "b2p_done", "dve_self", "pool_self", "act_self"]
        q = {n: sem(n) for n in names}
        part_w = [sem(f"part_w{i}") for i in range(2)]
        stack_in = [sem(f"stack_in{i}") for i in range(ROTS)]
        stored = [sem(f"stored{i}") for i in range(2)]
        mrow_in = [sem(f"mrow_in{i}") for i in range(2)]

        psF = (psS[0], psS[1], psE[0])
        block = ctx.enter_context(nc.Block())
        ROT = lambda b: b % ROTS

        def batch_at(t, offset):
            k = t - offset
            return k // G if k >= 0 and k % G == 0 and k // G < B else None

        def lagged(t, lag):
            k = t - lag
            return (k // G, k % G, k) if 0 <= k < B * G else (None, None, None)

        def sel_bit(t):
            n = t - SEL0
            return n if 0 <= n < NBITS else None

        SETS = {}
        count = 0
        for name, k in (("onehot", 1), ("sil1", 1), ("sil2", 1), ("silu", 1), ("wq", 1), ("wk", 1), ("wv", 1),
                        ("wo", 1), ("cols", 1), ("wrg", 1), ("beta", 1), ("sa", 1), ("modT", 1),
                        ("absg", 1), ("maxg", 1), ("sgn", 1), ("sgn2", 1), ("gates", 1), ("cb", 1), ("rows", 1), ("gs", 1), ("all", 1)):
            count += k
            SETS[name] = count

        @block.sync
        def _(sp):
            sp.dma_start(c_in[:, :], c).then_inc(q["c_in"], 16)
            sp.dma_start(x_all[:, 0], x[0].rearrange("(i p) d -> p i d", p=P)).then_inc(x_in[0], 16)
            sp.dma_start(wmod_sb[:, :], wmod).then_inc(q["wmod_in"], 16)
            for b in range(1, 3):
                sp.dma_start(x_all[:, b], x[b].rearrange("(i p) d -> p i d", p=P)).then_inc(x_in[b], 16)

            sp.dma_start(w1_sb[:, :], w1).then_inc(q["w1_in"], 16)
            sp.dma_start(w2_sb[:, :, :], w2.rearrange("(c p) d -> p c d", p=P)).then_inc(q["w2_in"], 16)

            def load_rest():
                for b in range(3, B):
                    sp.dma_start(x_all[:, b], x[b].rearrange("(i p) d -> p i d", p=P)).then_inc(x_in[b], 16)
                sp.dma_start(b1_bc[:, :], b1.partition_broadcast(P)).then_inc(q["bc_in"], 16)
                sp.dma_start(b2_bc[:, :], b2.partition_broadcast(P)).then_inc(q["bc_in"], 16)

            def stack(b):
                i = b % 2
                sp.wait_ge(q["split_done"], b + 1)
                sp.dma_start(parts_dram[b, 0:6].rearrange("s p t -> p s t"), part8[:, i]).then_inc(part_w[i], 16)
                sp.dma_start(parts_dram[b, 6:8].rearrange("s p t -> p s t"), part8[:, i, 3:5]).then_inc(part_w[i], 16)
                if b >= ROTS:
                    sp.wait_ge(q["e_done"], 3 * G * (b - ROTS + 1))
                sp.wait_ge(part_w[i], 32 * (b // 2 + 1))
                rowsz = NPART * HD
                for r in range(3):
                    sp.dma_start(Qs[rowsz * r:rowsz * (r + 1), ROT(b)],
                                 parts_dram[b, 0:3].rearrange("s (d h) t -> (s d) h t", d=HD)).then_inc(stack_in[ROT(b)], 16)
                    sp.dma_start(Ks[rowsz * r:rowsz * (r + 1), ROT(b)],
                                 parts_dram[b, 3 + r:6 + r].rearrange("s (d h) t -> (s d) h t", d=HD)).then_inc(stack_in[ROT(b)], 16)

            def mrows(b):
                sp.wait_ge(q["nmlo_done"], b + 1)
                sp.dma_start(Qs[R_S:R_S + 1, ROT(b)], nmT[:, b % 2, 0, :]).then_inc(mrow_in[b % 2], 16)
                sp.dma_start(Qs[R_S + 1:R_E, ROT(b)], nmT[:, b % 2, 1, :]).then_inc(mrow_in[b % 2], 16)

            for t in range(T_END):
                b = batch_at(t, AT_NMT)
                if b is not None:
                    mrows(b)
                b = batch_at(t, AT_SPLIT)
                if b is not None:
                    stack(b)
                    if b == 0:
                        load_rest()
            for p in range(NPAIR):
                sp.wait_ge(q["ob_done"], p + 1)
                sp.dma_start(out[2 * p:2 * p + 2].rearrange("b (i t) d -> t (b i) d", t=P), ob[:, p % 2]).then_inc(stored[p % 2], 16)
            for s in stored:
                sp.wait_ge(s, 16 * NPAIR // 2)

        @block.gpsimd
        def _(gp):
            gp.memset(ones_b[:, :], 1.0).then_inc(q["pool_set"], 1)
            gp.memset(mhalf[:, :], -0.5).then_inc(q["pool_set"], 1)
            for i in range(4):
                gp.memset(Vx[:, i], 1.0).then_inc(q["pool_set"], 1)
            gp.memset(beta_w[:, :], 1.0).then_inc(q["pool_set"], 1)
            for col, k in enumerate((K_STAT - 1, P * FF - K_STAT,
                                     2 * (P * FF - K_STAT) - P * FF, 2 * (K_STAT - 1) - P * FF)):
                gp.memset(ktab[:, col:col + 1], float(k)).then_inc(q["pool_set"], 1)

            def rstd(n0, n1_, k):
                gp.wait_ge(q["ln_stat"], k)
                gp.tensor_scalar(ve1[:, n0:n1_], mv1[:, n0:n1_, 1], EPS, None, op0=ALU.add).then_inc(q["pool_self"], 1)
                gp.wait_ge(q["pool_self"], k)
                gp.tensor_tensor(rs1[:, n0:n1_], ve1[:, n0:n1_], mhalf[:, n0:n1_], op=ALU.pow).then_inc(q["ln_rstd"], 1)

            def c_pool(p):
                own = B + 2 * p
                ks = slice(4 * p, 4 * p + 4)
                gp.wait_ge(q["ln2_stat"], p + 1)
                gp.tensor_scalar(ve1[:, ks], mv1[:, ks, 1], EPS, None, op0=ALU.add).then_inc(q["pool_self"], 1)
                gp.wait_ge(q["pool_self"], own + 1)
                gp.tensor_tensor(rs1[:, ks], ve1[:, ks], mhalf[:, ks], op=ALU.pow).then_inc(q["ln2_rstd"], 1)
                gp.wait_ge(q["ln3_stat"], p + 1)
                gp.tensor_scalar(ve3[:, ks], mv3[:, ks, 1], EPS, None, op0=ALU.add).then_inc(q["pool_self"], 1)
                gp.wait_ge(q["pool_self"], own + 2)
                gp.tensor_tensor(rs3[:, ks], ve3[:, ks], mhalf[:, ks], op=ALU.pow).then_inc(q["ln3_rstd"], 1)

            def c_exp(p):
                gp.wait_ge(q["logit_done"], p + 1)
                gp.tensor_tensor(ex[:, :, :], eul[:, :, :], lg[:, :, :], op=ALU.pow).then_inc(q["ex_done"], 1)

            gp.memset(eul[:, :, :], math.e).then_inc(q["pool_set"], 1)
            gp.wait_ge(q["pool_set"], POOL_SETS)
            rstd(0, NBLK, 1)
            def rot(a):
                return a.rearrange("r (h t) -> r h t", h=NH).unsqueeze(1).broadcast_to([a.shape[0], ROTS, NH, S])
            gp.dma_start(Qs[R_PROD:R_S], rot(q_const)).then_inc(q["const_in"], 16)
            gp.dma_start(Ks[R_PROD:R_E], rot(k_const)).then_inc(q["const_in"], 16)
            gp.dma_start(mask5[:, :, :], mask_c.rearrange("p (h k) -> p h k", h=HG + 1)).then_inc(q["const_in"], 16)
            gp.dma_start(vecs[0:NC, :], b1.rearrange("(c p) -> c p", p=P)).then_inc(q["vec_in"], 16)
            for r, vec in enumerate((b2, gamma, beta)):
                gp.dma_start(vecs[NC + r:NC + r + 1, :], vec.rearrange("(a n) -> a n", a=1)).then_inc(q["vec_in"], 16)
            gp.dma_start(wr_sb[:, :], wr).then_inc(q["vec_in"], 16)
            gp.dma_start(br_bc[:, :], br.partition_broadcast(P)).then_inc(q["vec_in"], 16)
            for t in range(T_END):
                if sel_bit(t) is not None:
                    n = sel_bit(t)
                    gp.wait_ge(q["cand_done"], n + 1)
                    if n:
                        gp.wait_ge(q["cnt_done"], n)
                    gp.tensor_scalar(msk[:, 1], w2a[:, :], cand[:, 1:2].bitcast(F32), None, op0=ALU.is_lt).then_inc(q["m_pool"], 1)
                b = batch_at(t, AT_QK)
                if b is not None and b + 1 < B:
                    rstd(NBLK * (b + 1), NBLK * (b + 2), b + 2)
                b, g, e = lagged(t, E_LAG)
                if b is not None:
                    for j in range(3):
                        gp.wait_ge(q["exp_done"], 3 * e + j + 1)
                        if j == 0:
                            v = PT[:, e % 2, 0].rearrange("p (h q) -> p h q", h=HG)
                        else:
                            v = PT[:, e % 2, j].rearrange("p (h q) -> p h q", h=2)[:, :, 0:P]
                        gp.affine_select(out=v, in_=v, compare_op=ALU.is_ge, fill=0.0, base=0,
                                         pattern=[[0, v.shape[1]], [1, P]], channel_multiplier=-1).then_inc(q["sel_done"], 1)
                if t in C_STEPS:
                    c_pool(C_STEPS[t])
            for p in range(NPAIR):
                c_exp(p)
                if p == 0:
                    c_pool(NPAIR - 1)

        @block.scalar
        def _(act):
            act.dma_start(ident[:, :], ident_c).then_inc(q["ident_in"], 16)
            act.dma_start(wqkv_in[:, :, :], w_qkv.rearrange("(j p) d -> p j d", p=P)).then_inc(q["qkvw_in"], 16)
            act.dma_start(wo_in[:, :], w_o).then_inc(q["qkvw_in"], 16)
            act.wait_ge(q["pe_set"], 1)
            act.activation(c_e[:, :], psQ[:, 0:B], ACT.Exp, scale=-1.0).then_inc(q["act_set"], 1)

            def exp_unit(t, j):
                b, g, e = lagged(t, E_LAG)
                if b is None:
                    return
                u = 3 * e + j
                act.wait_ge(q["e_done"], u + 1)
                if e >= 2 and j == 0:
                    act.wait_ge(q["pv_done"], e - 1)
                act.activation(PT[:, e % 2, j], psE[u % 2][:, :], ACT.Exp).then_inc(q["exp_done"], 1)

            def sign_mask(n, col, w):
                if n is None:
                    return
                act.wait_ge(q["cand_done"], n + 1)
                if n:
                    act.wait_ge(q["cnt_done"], n)
                act.activation(msk[:, col], w[:, :], ACT.Sign, bias=cand[:, col:col + 1].bitcast(F32),
                               scale=-(1.0 - 2.0 ** -24)).then_inc(q["m_act"], 1)

            def c_act_h(p):
                act.wait_ge(q["h2T_psum"], p + 1)
                if p >= 2:
                    act.wait_ge(q["f1_done"], 4 * 2 * (p - 1))
                    act.wait_ge(q["lgT_done"], p - 1)
                act.activation(h2T[:, p % 2], psE[1][:, :], ACT.Copy).then_inc(q["h2T_done"], 1)

            def c_act_l(p):
                act.wait_ge(q["lgT_done"], p + 1)
                if p:
                    act.wait_ge(q["lg_psum"], p)
                act.activation(lgT[:, :], psQ[0:NE, :], ACT.Copy).then_inc(q["lgT_out"], 1)

            def gelus(n):
                p, w = n // 2, n % 2
                for ch in range(NC):
                    act.wait_ge(q["f1_done"], 4 * n + ch + 1)
                    if n >= 2 and ch == 0:
                        act.wait_ge(q["f2_done"], n - 1)
                    if n == 1 and ch == 0:
                        act.wait_ge(q["b1p_done"], 1)
                    bias = b1p[:, ch:ch + 1] if w else cols[:, ch:ch + 1]
                    act.activation(hid[:, n % 2, ch, :], psF[(4 * n + ch) % 3][:, :], ACT.Gelu_apprx_tanh,
                                   bias=bias).then_inc(q["gelu_done"], 1)

            for t in range(T_END):
                n = sel_bit(t)
                if n == 0:
                    act.wait_ge(q["w1_in"], 16)
                    act.activation(w1a[:, :], w1_sb[:, :], ACT.Abs).then_inc(q["act_set"], 1)
                    act.wait_ge(q["w2_in"], 16)
                    act.activation(w2a[:, :], w2_sb.rearrange("p c d -> p (c d)"), ACT.Abs).then_inc(q["act_set"], 1)
                sign_mask(n, 2, w1a)
                b = batch_at(t, AT_NMT)
                if b is not None:
                    act.wait_ge(q["nmT_done"], b + 1)
                    if b >= 2:
                        act.wait_ge(mrow_in[b % 2], 32 * (b // 2))
                    act.activation(nmT[:, b % 2, 0, :], psX[0:NH, 0:S], ACT.Copy).then_inc(q["nmhi_done"], 1)
                b = batch_at(t, AT_OT)
                if b is not None:
                    act.wait_ge(q["at_done"], b + 1)
                    if b:
                        act.wait_ge(q["y_done"], b)
                    act.activation(AT[:, :], psX[:, 0:S], ACT.Copy).then_inc(q["at_out"], 1)
                b = batch_at(t, AT_V)
                if b is not None:
                    act.wait_ge(q["v_done"], b + 1)
                    if b == 0:
                        act.wait_ge(q["pool_set"], POOL_SETS)
                    if b >= 4:
                        act.wait_ge(q["pv_done"], G * (b - 3))
                    act.activation(Vx[:, b % 4, :, :, 0:HD],
                                   psX[:, 0:S].rearrange("p (i h d) -> p i h d", i=NBLK, h=NH),
                                   ACT.Copy).then_inc(q["v_out"], 1)
                sign_mask(n, 3, w2a)
                exp_unit(t, 0)
                exp_unit(t, 1)
                b, g, e = lagged(t, E_LAG + 1)
                if b is not None:
                    act.wait_ge(q["pv_done"], e + 1)
                    if e >= 2:
                        act.wait_ge(q["ut_done"], e - 1)
                    act.activation(U[:, e % 2], psO[:, 0:S], ACT.Copy).then_inc(q["u_done"], 1)
                exp_unit(t, 2)
                b = batch_at(t, AT_T)
                if b is not None:
                    act.wait_ge(q["t_done"], b + 1)
                    if b >= 2:
                        act.wait_ge(q["v_done"], b - 1)
                    if b == 0:
                        act.wait_ge(q["dve_set"], SETS["modT"])
                    act.activation(h1T[:, b % 2], psQ[:, 0:S], ACT.Identity, scale=modT[:, 1, b:b + 1],
                                   bias=modT[:, 0, b:b + 1]).then_inc(q["h1_done"], 1)
                b = batch_at(t, AT_QK)
                if b is not None:
                    act.wait_ge(q["qk_done"], b + 1)
                    if b >= 2:
                        act.wait_ge(part_w[b % 2], 32 * (b // 2))
                    act.activation(part8[:, b % 2, 0:4:3, :], psQ.rearrange("p (a t) -> p a t", a=2),
                                   ACT.Copy).then_inc(q["hi_done"], 1)
                for b in ROWS_AT.get(t, ()):
                    act.wait_ge(q["rb_done"], b + 1)
                    act.activation(rows_bc[:, b], (psO, psU)[b % 2][:, :].rearrange("p (r d) -> p r d", r=4), ACT.Copy).then_inc(q["rb_out"], 1)
                if t == FFN_STEP:
                    c_act_h(0)
                if t == FFN_STEP + 1:
                    c_act_l(0)
                    gelus(0)

            for n in range(1, 2 * NPAIR):
                gelus(n)
                if n % 2 and n // 2 + 1 < NPAIR:
                    c_act_h(n // 2 + 1)
                    c_act_l(n // 2 + 1)

        @block.tensor
        def _(pe):
            mm = nc.tensor.matmul
            tr = nc.tensor.transpose
            pe.wait_ge(q["c_in"], 16)
            pe.wait_ge(q["ident_in"], 16)
            tr(psQ[:, 0:B], c_in[:, :], ident[0:B, 0:B]).then_inc(q["pe_set"], 1)
            pe.wait_ge(q["qkvw_in"], 32)
            for j in range(3):
                tr(psS[0][:, j * P:(j + 1) * P], wqkv_in[:, j, :], ident[:, :])
            tr(psS[0][:, 3 * P:4 * P], wo_in[:, :], ident[:, :]).then_inc(q["pe_set"], 1)
            pe.wait_ge(q["vec_in"], 16 * 6)
            tr(psS[1][:, 0:NC + 3], vecs[:, :], ident[0:NC + 3, 0:NC + 3]).then_inc(q["pe_set"], 1)
            pe.wait_ge(q["dve_set"], SETS["silu"])
            pe.wait_ge(q["wmod_in"], 16)
            for j in range(2):
                mm(psE[0][:, j * B:(j + 1) * B], wmod_sb[:, j * D:(j + 1) * D], c_s[:, :], start=True, stop=True)
            mm(psE[1][0:B, 0:512], c_s[:, :], wmod_sb[:, 2 * D:6 * D], start=True, stop=True).then_inc(q["pe_set"], 1)
            pe.wait_ge(q["pool_set"], POOL_SETS)
            pe.wait_ge(q["dve_set"], SETS["wrg"])
            mm(psO[:, 0:NE], beta_w[:, :], wrg[:, :], start=True, stop=True)
            pe.wait_ge(q["dve_set"], SETS["beta"])
            mm(psO[:, NE:2 * NE], woTg[:, 0, :], wr_sb[:, :], start=True, stop=True).then_inc(q["pe_set"], 1)

            def s_unit(t, j):
                b, g, m = lagged(t, M_LAG)
                if b is None:
                    return
                u, r, bank = 3 * m + j, ROT(b), psS[(3 * m + j) % 2]
                if m == 0 and j == 0:
                    pe.wait_ge(q["const_in"], 16 * 3)
                    pe.wait_ge(q["dve_set"], SETS["all"])
                if g == 0 and j == 0:
                    pe.wait_ge(stack_in[r], 96 * (b // ROTS + 1))
                if u >= 2:
                    pe.wait_ge(q["max_done"], u - 1)
                if j == 0:
                    mm(bank[:, :], mask5[:, HG, :], mask5[:, 0:HG, :].rearrange("p h k -> p (h k)"), start=True, stop=False, skip_group_check=True)
                    for i in range(HG):
                        h = HG * g + i
                        last = mm(bank[:, i * P:(i + 1) * P], Qs[0:R_S, r, h, 0:P], Ks[0:R_S, r, h, 0:P],
                                  start=False, stop=True, skip_group_check=True)
                else:
                    mm(bank.rearrange("p (h k) -> p h k", h=2)[:, :, P:S], mask5[:, HG, :], mask5[:, 0:2, :],
                       start=True, stop=False, skip_group_check=True)
                    for i in range(2):
                        h = HG * g + 2 * (j - 1) + i
                        last = mm(bank[:, i * S:(i + 1) * S], Qs[0:R_S, r, h, P:S], Ks[0:R_S, r, h, :],
                                  start=False, stop=True, skip_group_check=True)
                last.then_inc(q["s_done"], 1)

            def e_unit(t, j):
                b, g, e = lagged(t, E_LAG)
                if b is None:
                    return
                u, r, bank = 3 * e + j, ROT(b), psE[(3 * e + j) % 2]
                if g == 0 and j == 0:
                    pe.wait_ge(mrow_in[b % 2], 32 * (b // 2 + 1))
                if u >= 2:
                    pe.wait_ge(q["exp_done"], u - 1)
                if j == 0:
                    for i in range(HG):
                        h = HG * g + i
                        last = mm(bank[:, i * P:(i + 1) * P], Ks[0:R_E, r, h, P:S], Qs[0:R_E, r, h, P:S],
                                  start=True, stop=True, skip_group_check=True)
                else:
                    for i in range(2):
                        h = HG * g + 2 * (j - 1) + i
                        last = mm(bank[:, i * S:(i + 1) * S], Ks[0:R_E, r, h, 0:P], Qs[0:R_E, r, h, :],
                                  start=True, stop=True, skip_group_check=True)
                last.then_inc(q["e_done"], 1)

            def pv(t):
                b, g, e = lagged(t, E_LAG + 1)
                if b is None:
                    return
                pe.wait_ge(q["sel_done"], 3 * e + 3)
                if g == 0:
                    pe.wait_ge(q["v_out"], b + 1)
                if e == 0:
                    pe.wait_ge(q["rb_out"], B)
                if e:
                    pe.wait_ge(q["u_done"], e)
                pt0 = PT[:, e % 2, 0].rearrange("p (h q) -> p h q", h=HG)
                for i in range(HG):
                    h = HG * g + i
                    mm(psO[32 * i:32 * i + 32, 0:S], Vx[:, b % 4, 0, h, :],
                       PT[:, e % 2, 1 + i // 2, (i % 2) * S:(i % 2 + 1) * S], start=True, stop=False,
                       skip_group_check=True)
                for i in range(HG):
                    h = HG * g + i
                    last = mm(psO[32 * i:32 * i + 32, P:S], Vx[:, b % 4, 1, h, :], pt0[:, i, :],
                              start=False, stop=True, skip_group_check=True)
                last.then_inc(q["pv_done"], 1)

            def ut(t):
                b, g, e = lagged(t, E_LAG + 1)
                if b is None:
                    return
                pe.wait_ge(q["u_done"], e + 1)
                if e:
                    pe.wait_ge(q["a_done"], e)
                for i in range(NBLK):
                    last = tr(psU[:, i * P:(i + 1) * P], U[:, e % 2, i * P:(i + 1) * P], ident[:, :])
                last.then_inc(q["ut_done"], 1)

            free_x = [None]

            def claim_x(reader):
                if free_x[0]:
                    pe.wait_ge(*free_x[0])
                free_x[0] = reader

            def c_pe_h(p):
                pe.wait_ge(q["h2_done"], p + 1)
                if p:
                    pe.wait_ge(q["h2T_done"], p)
                for i in range(4):
                    last = tr(psE[1][:, i * P:(i + 1) * P], h2[:, p, i, :], ident[:, :])
                last.then_inc(q["h2T_psum"], 1)

            def c_pe_l(p):
                pe.wait_ge(q["h2T_done"], p + 1)
                if p:
                    pe.wait_ge(q["lgT_out"], p)
                mm(psQ[0:NE, :], wrg[:, :], h2T[:, p % 2], start=True, stop=True).then_inc(q["lgT_done"], 1)

            def c_pe_t(p):
                pe.wait_ge(q["lgT_out"], p + 1)
                claim_x((q["lg_read"], p + 1))
                for i in range(4):
                    last = tr(psX[:, i * NE:(i + 1) * NE], lgT[:, i * P:(i + 1) * P], ident[0:NE, 0:NE])
                last.then_inc(q["lg_psum"], 1)

            def f1(n):
                p, w = n // 2, n % 2
                wt = w1p if w else w1_sb
                if w == 0:
                    pe.wait_ge(q["h2T_done"], p + 1)
                if n == 1:
                    pe.wait_ge(q["pert_done"], 1)
                for ch in range(NC):
                    k = 4 * n + ch
                    if k == 0:
                        pe.wait_ge(q["max_done"], 3 * G * B)
                        pe.wait_ge(q["exp_done"], 3 * G * B)
                    if k >= 3:
                        pe.wait_ge(q["gelu_done"], k - 2)
                    mm(psF[k % 3][:, :], wt[:, ch * P:(ch + 1) * P], h2T[:, p % 2], start=True, stop=True).then_inc(q["f1_done"], 1)

            def f2(n):
                p, w = n // 2, n % 2
                wt, bank = (w2p, psU) if w else (w2_sb, psO)
                if p:
                    pe.wait_ge(q["y_read"], n - 1)
                if n == 1:
                    pe.wait_ge(q["pert_done"], 2)
                pe.wait_ge(q["gelu_done"], 4 * (n + 1))
                for i in range(4):
                    for ch in range(NC):
                        last = mm(bank[:, i * P:(i + 1) * P], hid[:, n % 2, ch, i * P:(i + 1) * P], wt[:, ch, :],
                                  start=(ch == 0), stop=(ch == NC - 1), skip_group_check=True)
                last.then_inc(q["f2_done"], 1)

            for t in range(T_END):
                n = sel_bit(t)
                if t == B2_STEP:
                    pe.wait_ge(q["b2m_done"], 1)
                    claim_x((q["b2p_done"], 1))
                    mm(psX[:, 0:2 * P], ones_b[:, :], msk[:, 2, 0:2 * P], start=True, stop=True).then_inc(q["b2rank"], 1)
                b = batch_at(t, AT_NMT)
                if b is not None:
                    pe.wait_ge(q["max_done"], 3 * G * (b + 1))
                    claim_x((q["nmlo_done"], b + 1))
                    for i in range(NBLK):
                        last = tr(psX[0:NH, i * P:(i + 1) * P], nmax[:, b % 2, i, :], ident[:, :])
                    last.then_inc(q["nmT_done"], 1)
                b = batch_at(t, AT_V)
                if b is not None:
                    claim_x((q["v_out"], b + 1))
                    for i in range(NBLK):
                        last = mm(psX[:, i * P:(i + 1) * P], h1T[:, b % 2, i * P:(i + 1) * P], wvT[:, :], start=True, stop=True)
                    last.then_inc(q["v_done"], 1)
                b = batch_at(t, AT_OT)
                if b is not None:
                    pe.wait_ge(q["a_done"], G * (b + 1))
                    claim_x((q["at_out"], b + 1))
                    for i in range(NBLK):
                        last = tr(psX[:, i * P:(i + 1) * P], A[:, b % 2, i, :], ident[:, :])
                    last.then_inc(q["at_done"], 1)
                b = batch_at(t, AT_Y)
                if b is not None:
                    pe.wait_ge(q["wog_done"], b + 1)
                    claim_x((q["x2_done"], b + 1))
                    for i in range(NBLK):
                        last = mm(psX[:, i * P:(i + 1) * P], AT[:, i * P:(i + 1) * P], woTg[:, b, :], start=True, stop=True)
                    last.then_inc(q["y_done"], 1)
                s_unit(t, 0)
                e_unit(t, 0)
                s_unit(t, 1)
                e_unit(t, 1)
                pv(t)
                if n is not None:
                    pe.wait_ge(q["m_dve"], n + 1)
                    pe.wait_ge(q["m_act"], 2 * n + 2)
                    pe.wait_ge(q["m_pool"], n + 1)
                    claim_x((q["cnt_out"], n + 1))
                    for col in range(4):
                        for ch in range(NC):
                            last = mm(psX[:, col * NC + ch:col * NC + ch + 1], msk[:, col, ch * P:(ch + 1) * P],
                                      ones_b[:, 0:1], start=True, stop=True, skip_group_check=True)
                    last.then_inc(q["cnt_done"], 1)
                s_unit(t, 2)
                if n is not None:
                    claim_x((q["cond_done"], n + 1))
                    for ch in range(NC):
                        last = mm(psX[:, 0:4], ones_b[:, :], cnt[:, :, ch], start=(ch == 0), stop=(ch == NC - 1))
                    last.then_inc(q["tot_done"], 1)
                e_unit(t, 2)
                ut(t)
                b = batch_at(t, AT_T)
                if b is not None:
                    pe.wait_ge(q["n1_done"], b + 1)
                    if b == 0:
                        pe.wait_ge(q["dve_set"], SETS["silu"])
                    else:
                        pe.wait_ge(q["res_done"], b)
                    for i in range(NBLK):
                        last = tr(psQ[:, i * P:(i + 1) * P], n1[:, b % 2, i, :], ident[:, :])
                    last.then_inc(q["t_done"], 1)
                b = batch_at(t, AT_QK)
                if b is not None:
                    pe.wait_ge(q["h1_done"], b + 1)
                    for a in range(2):
                        last = mm(psQ[:, a * S:(a + 1) * S], wqkT[:, a, :], h1T[:, b % 2], start=True, stop=True)
                    last.then_inc(q["qk_done"], 1)
                for b in ROWS_AT.get(t, ()):
                    if b == 0:
                        pe.wait_ge(q["dve_set"], SETS["all"])
                    if b >= 2:
                        pe.wait_ge(q["rb_out"], b - 1)
                    mm((psO, psU)[b % 2][:, :], onehot[:, b, :], rows.rearrange("b r d -> b (r d)"), start=True, stop=True).then_inc(q["rb_done"], 1)

                if t == FFN_STEP:
                    pe.wait_ge(q["exp_done"], 3 * G * B)
                    c_pe_h(0)
                if t == FFN_STEP + 1:
                    c_pe_l(0)
                    f1(0)
            pe.wait_ge(q["a_done"], G * B)
            c_pe_t(0)
            for n in range(1, 2 * NPAIR + 1):
                if n < 2 * NPAIR:
                    f1(n)
                if n % 2 == 0 and n // 2 < NPAIR:
                    c_pe_t(n // 2)
                if n % 2 and (n + 1) // 2 < NPAIR:
                    c_pe_h((n + 1) // 2)
                f2(n - 1)
                if n % 2 and (n + 1) // 2 < NPAIR:
                    c_pe_l((n + 1) // 2)

        @block.vector
        def _(v):
            ve = nc.vector
            own = [0]

            def then_self(inst):
                own[0] += 1
                inst.then_inc(q["dve_self"], 1)
                v.wait_ge(q["dve_self"], own[0])

            def absolute(dst, src):
                return ve.tensor_scalar(dst.bitcast(U32), src.bitcast(U32), 0x7FFFFFFF, None, op0=ALU.bitwise_and)

            def ln1(b):
                v.wait_ge(x_in[b], 16)
                for i in range(NBLK):
                    last = ve.bn_stats(st1[:, 2 * b + i, :], x_all[:, b, i, :])
                then_self(last)
                for i in range(NBLK):
                    last = ve.bn_aggr(mv1[:, 2 * b + i, :], st1[:, 2 * b + i, :])
                last.then_inc(q["ln_stat"], 1)

            ln1(0)
            v.wait_ge(q["ident_in"], 16)
            ds = lambda inst: inst.then_inc(q["dve_set"], 1)
            ds(ve.tensor_copy(onehot[:, :, :], ident[0:B, 0:B].unsqueeze(2).broadcast_to([B, B, P])))
            v.wait_ge(q["act_set"], 1)
            ds(ve.tensor_scalar(c_e[:, :], c_e[:, :], 1.0, None, op0=ALU.add))
            v.wait_ge(q["dve_set"], SETS["sil1"])
            ds(ve.reciprocal(c_e[:, :], c_e[:, :]))
            v.wait_ge(q["dve_set"], SETS["sil2"])
            ds(ve.tensor_tensor(c_s[:, :], psQ[:, 0:B], c_e[:, :], op=ALU.mult))
            v.wait_ge(q["pe_set"], 2)
            ds(ve.tensor_scalar(wqkT[:, 0, :].rearrange("p (d h) -> p h d", d=HD),
                                psS[0][:, 0:P].rearrange("p (h d) -> p h d", h=NH), float(HD) ** -0.5, None, op0=ALU.mult))
            ds(ve.tensor_copy(wqkT[:, 1, :].rearrange("p (d h) -> p h d", d=HD),
                              psS[0][:, P:2 * P].rearrange("p (h d) -> p h d", h=NH)))
            ds(ve.tensor_copy(wvT[:, :], psS[0][:, 2 * P:3 * P]))
            ds(ve.tensor_copy(woT[:, :], psS[0][:, 3 * P:4 * P]))
            v.wait_ge(q["pe_set"], 3)
            ds(ve.tensor_copy(cols[:, :], psS[1][:, 0:NC + 3]))
            v.wait_ge(q["dve_set"], SETS["cols"])
            ds(ve.tensor_scalar(wrg[:, :], wr_sb[:, :], cols[:, NC + 1:NC + 2], None, op0=ALU.mult))
            ds(ve.tensor_copy(woTg[:, 0, :], cols[:, NC + 2:NC + 3].broadcast_to([P, P])))
            v.wait_ge(q["pe_set"], 4)
            ds(ve.tensor_copy(modT[:, 0, :], psE[0][:, 0:B]))
            ds(ve.tensor_scalar(modT[:, 1, :], psE[0][:, B:2 * B], 1.0, None, op0=ALU.add))
            pg = psE[1][0:B, :].rearrange("b (r d) -> b r d", r=4)
            ds(absolute(rows[:, 0:2, :], pg[:, 0:4:3, :]))
            v.wait_ge(q["dve_set"], SETS["absg"])
            ds(ve.tensor_scalar(rows[:, 0:2, :], rows[:, 0:2, :], 0.25, None, op0=ALU.max))
            ds(ve.tensor_scalar(rowt[:, :, :], pg[:, 0:4:3, :], 0.0, 2.0, op0=ALU.is_ge, op1=ALU.mult))
            v.wait_ge(q["dve_set"], SETS["sgn"])
            ds(ve.tensor_scalar(rowt[:, :, :], rowt[:, :, :], -1.0, None, op0=ALU.add))
            v.wait_ge(q["dve_set"], SETS["sgn2"])
            ds(ve.tensor_tensor(rows[:, 0:2, :], rows[:, 0:2, :], rowt[:, :, :], op=ALU.mult))
            ds(ve.tensor_scalar(rows[:, 2, :], pg[:, 2, :], 1.0, None, op0=ALU.add))
            ds(ve.tensor_copy(rows[:, 3, :], pg[:, 1, :]))
            v.wait_ge(q["pe_set"], 5)
            ds(ve.tensor_copy(gsum[:, 0:NE], psO[:, 0:NE]))
            ds(ve.tensor_tensor(gsum[:, NE:2 * NE], psO[:, NE:2 * NE], br_bc[:, :], op=ALU.add))
            v.wait_ge(q["pool_set"], POOL_SETS)

            def or_next(dst, n):
                bit = 1 << (NBITS - 1 - n)
                ve.tensor_scalar(dst[:, 0:2], cur[:, 0:2], bit, None, op0=ALU.bitwise_or)
                return ve.tensor_scalar(dst[:, 2:4], cur[:, 2:4], bit - 1, None, op0=ALU.bitwise_or)

            def first_cand():
                then_self(ve.memset(cur[:, :], 0))
                v.wait_ge(q["act_set"], 3)
                then_self(or_next(cand, 0))
                or_next(nxt, 1).then_inc(q["cand_done"], 1)

            def update(n):
                bit = NBITS - 1 - n
                v.wait_ge(q["tot_done"], n + 1)
                ve.tensor_tensor(cond[:, :], psX[:, 0:4], ktab[:, :], op=ALU.is_le).then_inc(q["cond_done"], 1)
                v.wait_ge(q["cond_done"], n + 1)
                if bit:
                    ve.scalar_tensor_tensor(cand[:, :], cond[:, :], bit, nxt[:, :], op0=ALU.logical_shift_left,
                                            op1=ALU.bitwise_or).then_inc(q["cand_done"], 1)
                inst = ve.scalar_tensor_tensor(cur[:, :], cond[:, :], bit, cur[:, :], op0=ALU.logical_shift_left, op1=ALU.bitwise_or)
                if bit:
                    then_self(inst)
                else:
                    inst.then_inc(q["cand_done"], 1)
                if bit > 1:
                    then_self(or_next(nxt, n + 2))

            def dve_mask(n):
                v.wait_ge(q["cand_done"], n + 1)
                ve.tensor_scalar(msk[:, 0], w1a[:, :], cand[:, 0:1].bitcast(F32), None, op0=ALU.is_lt).then_inc(q["m_dve"], 1)

            def maxima(t, j):
                b, g, m = lagged(t, M_LAG)
                if b is None:
                    return
                if g == 0 and j == 0 and b >= 2:
                    v.wait_ge(q["nmT_done"], b - 1)
                v.wait_ge(q["s_done"], 3 * m + j + 1)
                bank = psS[(3 * m + j) % 2]
                if j == 0:
                    ve.tensor_reduce(nmax[:, b % 2, 0, HG * g:HG * (g + 1)], bank.rearrange("p (h k) -> p h k", h=HG),
                                     axis=AX.X, op=ALU.max, negate=True).then_inc(q["max_done"], 1)
                else:
                    h = HG * g + 2 * (j - 1)
                    ve.tensor_reduce(nmax[:, b % 2, 1, h:h + 2], bank.rearrange("p (h k) -> p h k", h=2),
                                     axis=AX.X, op=ALU.max, negate=True).then_inc(q["max_done"], 1)

            def c_ln(p):
                xp = x_all[:, 2 * p:2 * p + 2].rearrange("p b i d -> p (b i) d")
                v.wait_ge(q["x2_done"], 2 * p + 2)
                for i in range(4):
                    last = ve.bn_stats(st1[:, 4 * p + i, :], xp[:, i, :])
                then_self(last)
                for i in range(4):
                    last = ve.bn_aggr(mv1[:, 4 * p + i, :], st1[:, 4 * p + i, :])
                last.then_inc(q["ln2_stat"], 1)
                v.wait_ge(q["ln2_rstd"], p + 1)
                for i in range(4):
                    k = 4 * p + i
                    last = ve.tensor_scalar(n2[:, i, :], xp[:, i, :], mv1[:, k, 0:1], rs1[:, k:k + 1],
                                            op0=ALU.subtract, op1=ALU.mult)
                then_self(last)
                v.wait_ge(q["rb_out"], B)
                for r, src in ((2, n2), (3, h2[:, p])):
                    for k in range(2):
                        ks = slice(2 * k, 2 * k + 2)
                        last = ve.tensor_tensor(h2[:, p, ks, :], src[:, ks, :],
                                                rows_bc[:, 2 * p + k, r, :].unsqueeze(1).broadcast_to([P, NBLK, D]),
                                                op=ALU.mult if r == 2 else ALU.add)
                    if r == 2:
                        then_self(last)
                last.then_inc(q["h2_done"], 1)
                v.wait_ge(q["h2_done"], p + 1)
                for i in range(4):
                    last = ve.bn_stats(st1[:, 4 * p + i, :], h2[:, p, i, :])
                then_self(last)
                for i in range(4):
                    last = ve.bn_aggr(mv3[:, 4 * p + i, :], st1[:, 4 * p + i, :])
                last.then_inc(q["ln3_stat"], 1)

            def router(p):
                ks = slice(4 * p, 4 * p + 4)
                e8 = lambda a: a.unsqueeze(2).broadcast_to([P, 4, NE])
                g8 = lambda a: a.unsqueeze(1).broadcast_to([P, 4, NE])
                v.wait_ge(q["ln3_stat"], p + 1)
                then_self(ve.tensor_tensor(lt[:, :, :], e8(mv3[:, ks, 0]), g8(gsum[:, 0:NE]), op=ALU.mult))
                v.wait_ge(q["lg_psum"], p + 1)
                ve.tensor_tensor(lg[:, :, :], psX[:, 0:4 * NE].rearrange("p (i e) -> p i e", i=4), lt[:, :, :],
                                 op=ALU.subtract).then_inc(q["lg_read"], 1)
                v.wait_ge(q["lg_read"], p + 1)
                v.wait_ge(q["ln3_rstd"], p + 1)
                then_self(ve.tensor_tensor(lg[:, :, :], lg[:, :, :], e8(rs3[:, ks]), op=ALU.mult))
                then_self(ve.tensor_tensor(lg[:, :, :], lg[:, :, :], g8(gsum[:, NE:2 * NE]), op=ALU.add))
                then_self(ve.tensor_reduce(lmax[:, :], lg[:, :, :], axis=AX.X, op=ALU.max))
                ve.tensor_tensor(lg[:, :, :], lg[:, :, :], e8(lmax[:, :]), op=ALU.subtract).then_inc(q["logit_done"], 1)
                v.wait_ge(q["ex_done"], p + 1)
                ve.tensor_reduce(esum[:, :], ex[:, :, :], axis=AX.X, op=ALU.add)
                then_self(ve.tensor_reduce(esum1[:, :], ex[:, :, 1:NE], axis=AX.X, op=ALU.add))
                then_self(ve.reciprocal(esum[:, :], esum[:, :]))
                ve.tensor_tensor(pr[:, p % 2, 0, :], ex[:, :, 0], esum[:, :], op=ALU.mult)
                then_self(ve.tensor_tensor(pr[:, p % 2, 1, :], esum1[:, :], esum[:, :], op=ALU.mult))
                if p:
                    v.wait_ge(q["ob_done"], p)
                for w in range(2):
                    last = ve.tensor_tensor(yt[:, w], (b2p_bc if w else b2_bc)[:, :].unsqueeze(1).broadcast_to([P, 4, D]),
                                            pr[:, p % 2, w, :].unsqueeze(2).broadcast_to([P, 4, D]), op=ALU.mult)
                then_self(last)
                then_self(ve.tensor_tensor(yt[:, 1], yt[:, 1], yt[:, 0], op=ALU.add))

            def combine(n):
                p, w = n // 2, n % 2
                bank = (psU if w else psO).rearrange("p (i d) -> p i d", i=4)
                v.wait_ge(q["f2_done"], n + 1)
                for i in range(4):
                    last = ve.scalar_tensor_tensor(yt[:, w, i], bank[:, i], pr[:, p % 2, w, i:i + 1], yt[:, 1 - w, i],
                                                   op0=ALU.mult, op1=ALU.add)
                last.then_inc(q["y_read"], 1)
                v.wait_ge(q["y_read"], n + 1)
                if w:
                    for k in range(2):
                        bs = slice(2 * k, 2 * k + 2)
                        last = ve.tensor_tensor(yt[:, 1, bs], yt[:, 1, bs],
                                                rows_bc[:, 2 * p + k, 1, :].unsqueeze(1).broadcast_to([P, NBLK, D]), op=ALU.mult)
                    if p >= 2:
                        v.wait_ge(stored[p % 2], 16 * (p // 2))
                    then_self(last)
                    ve.tensor_tensor(ob[:, p % 2], yt[:, 1], x_all[:, 2 * p:2 * p + 2].rearrange("p b i d -> p (b i) d"),
                                     op=ALU.add).then_inc(q["ob_done"], 1)

            def perturb(w, a, top, bot, dst):
                t0, t1 = msk[:, 0], msk[:, 1]
                then_self(ve.tensor_scalar(t0, a, top.bitcast(F32), None, op0=ALU.is_ge))
                then_self(ve.scalar_tensor_tensor(t1, a, bot.bitcast(F32), t0, op0=ALU.is_le, op1=ALU.is_gt))
                then_self(ve.tensor_tensor(t1, t1, t0, op=ALU.subtract))
                then_self(ve.scalar_tensor_tensor(dst, w, 0.8, t1, op0=ALU.mult, op1=ALU.mult))
                ve.tensor_tensor(dst, dst, w, op=ALU.add).then_inc(q["pert_done"], 1)

            def tiers(low, high, w, dst, tmp, k, done):
                then_self(ve.tensor_scalar(tmp, high, float(k - 1), None, op0=ALU.is_le))
                then_self(ve.scalar_tensor_tensor(dst, low, float(k - 1), tmp, op0=ALU.is_le, op1=ALU.is_gt))
                then_self(ve.tensor_tensor(dst, dst, tmp, op=ALU.subtract))
                then_self(ve.scalar_tensor_tensor(dst, w, 0.8, dst, op0=ALU.mult, op1=ALU.mult))
                ve.tensor_tensor(dst, dst, w, op=ALU.add).then_inc(q[done], 1)

            def perturb_b1():
                then_self(absolute(colsa[:, :], cols[:, :]))
                then_self(absolute(b1a[:, :], b1_bc[:, :]))
                for ch in range(NC):
                    for k, op in enumerate((ALU.is_lt, ALU.is_gt)):
                        last = ve.tensor_scalar(msk[:, k], b1a[:, :], colsa[:, ch:ch + 1], None, op0=op, op1=ALU.add,
                                                accum_out=rank[:, k, ch:ch + 1])
                    then_self(last)
                tiers(rank[:, 0, :], rank[:, 1, :], cols[:, 0:NC], b1p[:, :], rtmp[:, :], K_B1, "b1p_done")
                then_self(absolute(b2a[:, :], b2_bc[:, :]))
                ve.tensor_scalar(msk[:, 2, 0:P], b2a[:, :], colsa[:, NC:NC + 1], None, op0=ALU.is_gt)
                ve.tensor_scalar(msk[:, 2, P:2 * P], b2a[:, :], colsa[:, NC:NC + 1], None, op0=ALU.is_lt).then_inc(q["b2m_done"], 1)

            def perturb_b2():
                v.wait_ge(q["b2rank"], 1)
                tiers(psX[:, 0:P], psX[:, P:2 * P], b2_bc[:, :], b2p_bc[:, :], b2t[:, :], K_B2, "b2p_done")

            for t in range(T_END):
                n = sel_bit(t)
                if t == SEL0:
                    first_cand()
                    dve_mask(0)
                if t == B2_STEP:
                    perturb_b2()
                maxima(t, 0)
                b = batch_at(t, AT_NMT)
                if b is not None:
                    v.wait_ge(q["nmhi_done"], b + 1)
                    ve.tensor_tensor(nmT[:, b % 2, 1, :], psX[0:NH, 0:S], nmT[:, b % 2, 0, :], op=ALU.subtract).then_inc(q["nmlo_done"], 1)
                b = batch_at(t, AT_Y)
                if b is not None:
                    v.wait_ge(q["y_done"], b + 1)
                    ve.tensor_tensor(x_all[:, b], x_all[:, b], psX[:, 0:S].rearrange("p (i d) -> p i d", i=NBLK),
                                     op=ALU.add).then_inc(q["x2_done"], 1)
                maxima(t, 1)
                if n is not None:
                    v.wait_ge(q["cnt_done"], n + 1)
                    ve.tensor_copy(cnt.rearrange("p a c -> p (a c)"), psX[:, 0:4 * NC]).then_inc(q["cnt_out"], 1)
                maxima(t, 2)
                if n is not None:
                    update(n)
                    if n + 1 < NBITS:
                        dve_mask(n + 1)
                b, g, e = lagged(t, E_LAG + 1)
                if b is not None:
                    v.wait_ge(q["ut_done"], e + 1)
                    pu = psU[:, 0:S].rearrange("p (i h r) -> p i h r", i=NBLK, h=HG)
                    then_self(ve.reciprocal(rden[:, :, :], pu[:, :, :, HD]))
                    if g == 0 and b >= 2:
                        v.wait_ge(q["at_done"], b - 1)
                    ve.tensor_tensor(A[:, b % 2, :, HG * HD * g:HG * HD * (g + 1)].rearrange("p i (h d) -> p i h d", h=HG),
                                     pu[:, :, :, 0:HD], rden[:, :, :].unsqueeze(3).broadcast_to([P, NBLK, HG, HD]),
                                     op=ALU.mult).then_inc(q["a_done"], 1)
                b = batch_at(t, AT_SPLIT)
                if b is not None:
                    i = b % 2
                    v.wait_ge(q["hi_done"], b + 1)
                    if b >= 2:
                        v.wait_ge(part_w[b % 2], 32 * (b // 2))
                    pq = psQ.rearrange("p (a t) -> p a t", a=2)
                    ve.tensor_tensor(resid[:, :, :], pq, part8[:, i, 0:4:3, :], op=ALU.subtract).then_inc(q["res_done"], 1)
                    v.wait_ge(q["res_done"], b + 1)
                    then_self(ve.tensor_copy(part8[:, i, 1:5:3, :], resid[:, :, :]))
                    ve.tensor_tensor(part8[:, i, 2:6:3, :], resid[:, :, :], part8[:, i, 1:5:3, :], op=ALU.subtract).then_inc(q["split_done"], 1)
                b = batch_at(t, AT_N1)
                if b is not None:
                    v.wait_ge(q["ln_rstd"], b + 1)
                    if b >= 2:
                        v.wait_ge(q["t_done"], b - 1)
                    for i in range(NBLK):
                        k = 2 * b + i
                        last = ve.tensor_scalar(n1[:, b % 2, i, :], x_all[:, b, i, :], mv1[:, k, 0:1], rs1[:, k:k + 1],
                                                op0=ALU.subtract, op1=ALU.mult)
                    last.then_inc(q["n1_done"], 1)
                b = batch_at(t, AT_T)
                if b is not None and b + 1 < B:
                    ln1(b + 1)
                for b in ROWS_AT.get(t - 1, ()):
                    v.wait_ge(q["rb_out"], b + 1)
                    if b == 0:
                        v.wait_ge(q["pe_set"], 5)
                    ve.tensor_tensor(woTg[:, b, :], woT[:, :], rows_bc[:, b, 0, :], op=ALU.mult).then_inc(q["wog_done"], 1)
                if t in C_STEPS:
                    c_ln(C_STEPS[t])
                if t == W1_STEP:
                    perturb(w1_sb[:, :], w1a[:, :], cur[:, 2:3], cur[:, 0:1], w1p[:, :])
                if t == W2_STEP:
                    flat = lambda a: a.rearrange("p c d -> p (c d)")
                    perturb(flat(w2_sb), w2a[:, :], cur[:, 1:2], cur[:, 3:4], flat(w2p))
                if t == B1_STEP:
                    v.wait_ge(q["bc_in"], 32)
                    perturb_b1()
            router(0)
            c_ln(NPAIR - 1)
            for n in range(2 * NPAIR):
                combine(n)
                if n % 2 and n // 2 + 1 < NPAIR:
                    router(n // 2 + 1)


def slopes():
    start = 2 ** (-2 ** (-(math.log2(NH) - 3)))
    return np.asarray([start * start ** i for i in range(NH)], np.float32)


def bf16_bits(a):
    return (np.ascontiguousarray(a, np.float32).view(np.uint32) >> 16).astype(np.uint16)


def constants():
    rest = slopes()
    sp = []
    for _ in range(3):
        part = (rest.view(np.uint32) & 0xFFFF0000).view(np.float32)
        sp.append(part)
        rest = rest - part
    pos = np.arange(S, dtype=np.float32)
    kc = np.ones((R_BIAS + R_MAX, NH, S), np.float32)
    qc = np.zeros((R_BIAS, NH, S), np.float32)
    for i in range(3):
        kc[i] = sp[i][:, None]
        qc[i] = pos[None, :]
        kc[3 + i] = pos[None, :]
        qc[3 + i] = -sp[i][:, None]
    above = np.where(np.arange(P)[None, :] > np.arange(P)[:, None], NEG, 0.0)
    mask = np.concatenate([above] * HG + [np.eye(P)], axis=1)
    return {"k_const": bf16_bits(kc.reshape(-1, NH * S)), "q_const": bf16_bits(qc.reshape(-1, NH * S)),
            "ident_c": np.eye(P, dtype=np.float32), "mask_c": bf16_bits(mask)}


_INS = [("L0_attn_x", "x"), ("L0_attn_W_qkv", "w_qkv"), ("L0_attn_W_o", "w_o"), ("L0_ffn_W1", "w1"), ("L0_ffn_b1", "b1"),
        ("L0_ffn_W2", "w2"), ("L0_ffn_b2", "b2"), ("L0_ffn_ln_gamma", "gamma"), ("L0_ffn_ln_beta", "beta"),
        ("L0_ffn_Wr", "wr"), ("L0_ffn_br", "br"), ("L0_c", "c"), ("L0_wmod", "wmod")]


def kernel(**inputs):
    import concourse.bacc as bacc
    from concourse.bass_utils import run_bass_kernel_spmd

    nc = bacc.Bacc("TRN2", target_bir_lowering=False, num_devices=1)
    arrays = {f"in_{short}": np.ascontiguousarray(inputs[name]) for name, short in _INS}
    arrays.update({f"in_{name}": a for name, a in constants().items()})
    args = [nc.dram_tensor(n, a.shape, mybir.dt.from_np(a.dtype), kind="ExternalInput").ap() for n, a in arrays.items()]
    parts = nc.dram_tensor("parts", [B, 8, P, S], BF16, kind="Internal").ap()
    out = nc.dram_tensor("out_0", [B, S, D], F32, kind="ExternalOutput").ap()
    args = [a.bitcast(BF16) if a.dtype == mybir.dt.uint16 else a for a in args]
    adaln_block(nc, *args, parts, out)
    r = run_bass_kernel_spmd(nc, [arrays], core_ids=[0])
    return r.results[0]["out_0"]
```

```python
from contextlib import ExitStack
import math

import numpy as np

import concourse.bass as bass
from concourse import mybir

F32 = mybir.dt.float32
BF16 = mybir.dt.bfloat16
U32 = mybir.dt.uint32
ALU = mybir.AluOpType
ACT = mybir.ActivationFunctionType
AX = mybir.AxisListType

P = 128
B, S, D = 8, 256, 128
NH, HD = 16, 8
NBLK = S // P
FF = 512
NC = FF // P
NE = 8
G = 4
HG = NH // G
NPART = 3
R_PROD = NPART * NPART * HD
R_BIAS = 6
R_MAX = 2
R_S = R_PROD + R_BIAS
R_E = R_S + R_MAX
M_LAG, E_LAG = 7, 12
SEL0 = 4
AT_N1, AT_T, AT_QK, AT_SPLIT = 0, 1, 2, 3
AT_LO, AT_V = 4, 4
AT_NMT = M_LAG + G
AT_OT, AT_Y = E_LAG + G + 1, E_LAG + G + 2
NBITS = 31
NEG = -1.0e30
EPS = 1e-5
ROTS = 3
K_STAT = int(P * FF * 0.1 / 2)
K_B1 = int(FF * 0.1 / 2)
K_B2 = int(D * 0.1 / 2)
ROWS_STEP, VEC_STEP, WO_STEP = 2, 3, 8
ROW_DMAS = 4
T_END = AT_Y + G * (B - 1) + 1
LN_STAT_AT = {37: 0, 40: 1, 43: 2}
LN_USE_AT = {39: 0, 41: 1, 44: 2}
LN_NEXT_AT = {40: 0, 42: 1, 45: 2}
W1_STEP, W2_STEP = 35, 42
B1_STEP, B1_USE = 25, 43
B2_STEP, B2_USE = 7, 10
FFN_STEP = E_LAG + B * G
FIRST_STEP = M_LAG + B * G + 1
NF = 4
assert T_END - FFN_STEP - 1 == NC // 2 and SEL0 + NBITS <= W1_STEP
assert B1_STEP + 2 * (2 * NC - 1) < B1_USE
assert all(AT_Y + G * (2 * p + 1) < t for t, p in LN_STAT_AT.items())
NPAIR = B // 2
POOL_SETS = 12


def adaln_block(nc, x, w_qkv, w_o, w1, b1, w2, b2, gamma, beta, wr, br, c, wmod,
                k_const, q_const, ident_c, mask_c, parts_dram, rows_dram, out):
    with ExitStack() as ctx:
        def sb(name, shape, dt=F32):
            return ctx.enter_context(nc.sbuf_tensor(name, shape, dt))

        def sem(name):
            return ctx.enter_context(nc.semaphore(name))

        x_all = sb("x_all", [P, B, NBLK, D])
        ident = sb("ident", [P, P])
        mask5 = sb("mask5", [P, HG + 1, P], BF16)
        ones_b = sb("ones_b", [P, P], BF16)
        wqkv_in = sb("wqkv_in", [P, 3, D])
        wo_in = sb("wo_in", [P, D])
        wqkT = sb("wqkT", [P, 2, D])
        wvT = sb("wvT", [P, D])
        woT = sb("woT", [P, D])
        woTg = sb("woTg", [P, B, D])
        w1_sb = sb("w1_sb", [P, FF])
        w2_sb = sb("w2_sb", [P, NC, D])
        w1p = sb("w1p", [P, FF])
        w2p = sb("w2p", [P, NC, D])
        w1a = sb("w1a", [P, FF])
        w2a = sb("w2a", [P, FF])
        b1_bc = sb("b1_bc", [P, FF])
        b2_bc = sb("b2_bc", [P, D])
        b2p_bc = sb("b2p_bc", [P, D])
        br_bc = sb("br_bc", [P, NE])
        vecs = sb("vecs", [NC + 3, P])
        cols = sb("cols", [P, NC + 3])
        colsa = sb("colsa", [P, NC + 3])
        b1p = sb("b1p", [P, NC])
        wr_sb = sb("wr_sb", [P, NE])
        wrg = sb("wrg", [P, NE])
        beta_w = sb("beta_w", [P, P])
        gsum = sb("gsum", [P, 2 * NE])
        c_in = sb("c_in", [B, D])
        c_e = sb("c_e", [P, B])
        c_s = sb("c_s", [P, B])
        wmod_sb = sb("wmod_sb", [P, 6 * D])
        modT = sb("modT", [P, 2, B])
        rows = sb("rows", [B, 4, D])
        rowt = sb("rowt", [B, 2, D])
        rows_bc = sb("rows_bc", [P, B, 4, D])
        st1 = sb("st1", [P, B * NBLK, 6])
        mv1 = sb("mv1", [P, B * NBLK, 2])
        ve1 = sb("ve1", [P, B * NBLK])
        rs1 = sb("rs1", [P, B * NBLK])
        mhalf = sb("mhalf", [P, B * NBLK])
        n1 = sb("n1", [P, 2, NBLK, D])
        h1T = sb("h1T", [P, 2, S])
        part8 = sb("part8", [P, 2, 6, S], BF16)
        resid = sb("resid", [P, 2, S])
        Qs = sb("Qs", [R_E, ROTS, NH, S], BF16)
        Ks = sb("Ks", [R_E, ROTS, NH, S], BF16)
        Vx = sb("Vx", [P, 4, NBLK, NH, 32])
        nmax = sb("nmax", [P, 2, NBLK, NH])
        nmT = sb("nmT", [NH, 2, R_MAX, S], BF16)
        PT = sb("PT", [P, 2, 3, HG * P])
        U = sb("U", [P, 2, S])
        rden = sb("rden", [P, NBLK, HG])
        A = sb("A", [P, 2, NBLK, D])
        AT = sb("AT", [P, S])
        msk = sb("msk", [P, 4, FF], BF16)
        cnt = sb("cnt", [P, 4, NC], BF16)
        ktab = sb("ktab", [P, 4])
        cond = sb("cond", [P, 4], U32)
        cur = sb("cur", [P, 4], U32)
        cand = sb("cand", [P, 4], U32)
        nxt = sb("nxt", [P, 4], U32)

        n2 = sb("n2", [P, 4, D])
        h2 = sb("h2", [P, NPAIR, 4, D])
        h2T = sb("h2T", [P, 2, 4 * P])
        mv3 = sb("mv3", [P, B * NBLK, 2])
        ve3 = sb("ve3", [P, B * NBLK])
        rs3 = sb("rs3", [P, B * NBLK])
        lgT = sb("lgT", [NE, 4 * P])
        lg = sb("lg", [P, 4, NE])
        lt = sb("lt", [P, 4, NE])
        ex = sb("ex", [P, 4, NE])
        eul = sb("eul", [P, 4, NE])
        lmax = sb("lmax", [P, 4])
        esum = sb("esum", [P, 4])
        esum1 = sb("esum1", [P, 4])
        pr = sb("pr", [P, 2, 2, 4])
        hid = sb("hid", [P, 2, NC, 4 * P])
        yt = sb("yt", [P, 2, 4, D])
        ob = sb("ob", [P, 2, 4, D])
        b1a = sb("b1a", [P, FF])
        b2a = sb("b2a", [P, D])
        b2t = sb("b2t", [P, D])
        b2m = sb("b2m", [P, 2, P], BF16)
        rmask = hid.rearrange("p a c t -> p (a c t)").bitcast(BF16).rearrange("p (m k c t) -> p m k c t", m=2, k=2, c=NC)[:, 1]
        rtmp = sb("rtmp", [P, NC])

        banks = [ctx.enter_context(nc.psum_tensor(f"bank{i}", [P, 512], F32)) for i in range(8)]
        psS, psE, psO, psU, psQ, psX = banks[0:2], banks[2:4], banks[4], banks[5], banks[6], banks[7]

        x_in = [sem(f"x_in{b}") for b in range(B)]
        names = ["qkvw_in", "c_in", "ident_in", "wmod_in", "vec_in", "w1_in", "w2_in", "const_in", "bc_in",
                 "pool_set", "dve_set", "act_set", "pe_set",
                 "ln_stat", "ln_rstd", "n1_done", "t_done", "h1_done", "qk_done", "v_done", "v_out",
                 "hi_done", "res_done", "mid_done", "split_done", "s_done", "max_done", "nmT_done", "nmhi_done",
                 "nmlo_done", "e_done", "exp_done", "sel_done", "pv_done", "u_done", "ut_done",
                 "rd_done", "a_done", "at_done", "at_out", "y_done", "x2_done", "rows_out",
                 "wog_done", "cand_done", "m_dve", "m_act", "m_pool", "cnt_done", "cnt_out",
                 "tot_done", "cond_done", "cur_done", "nxt_done", "ln2_stat", "ln2_rstd", "h2_done", "ln3_stat", "ln3_rstd",
                 "h2T_psum", "h2T_done", "lgT_done", "lgT_out", "lg_psum", "lg_read", "logit_done", "ex_done",
                 "f1_done", "f2_done", "gelu_done", "y_read", "ob_done", "pert_done", "b1p_done",
                 "b1abs_done", "b1m_done", "b1rank", "b2m_done", "b2rank", "b2p_done", "dve_self", "pool_self"]
        q = {n: sem(n) for n in names}
        part_w = [sem(f"part_w{i}") for i in range(2)]
        stack_in = [sem(f"stack_in{i}") for i in range(ROTS)]
        rows_in = [sem(f"rows_in{i}") for i in range(ROW_DMAS)]
        stored = [sem(f"stored{i}") for i in range(2)]
        mrow_in = [sem(f"mrow_in{i}") for i in range(2)]

        psF = (psS[0], psS[1], psQ, psE[0])
        assert len(psF) == NF
        block = ctx.enter_context(nc.Block())
        ROT = lambda b: b % ROTS

        def batch_at(t, offset):
            k = t - offset
            return k // G if k >= 0 and k % G == 0 and k // G < B else None

        def lo_at(t):
            return 0 if t == AT_SPLIT else batch_at(t, AT_LO) or None

        def lagged(t, lag):
            k = t - lag
            return (k // G, k % G, k) if 0 <= k < B * G else (None, None, None)

        def sel_bit(t):
            n = t - SEL0
            return n if 0 <= n < NBITS else None

        SETS = {name: k + 1 for k, name in enumerate((
            "sil1", "sil2", "silu", "wq", "wk", "wv", "wo", "sa", "modT", "absg", "maxg", "sgn", "sgn2",
            "gates", "cb", "rows", "cols", "wrg", "beta", "gs", "all"))}

        @block.sync
        def _(sp):
            sp.dma_start(c_in[:, :], c).then_inc(q["c_in"], 16)
            sp.dma_start(x_all[:, 0], x[0].rearrange("(i p) d -> p i d", p=P)).then_inc(x_in[0], 16)
            sp.dma_start(wmod_sb[:, :], wmod).then_inc(q["wmod_in"], 16)
            for b in range(1, 3):
                sp.dma_start(x_all[:, b], x[b].rearrange("(i p) d -> p i d", p=P)).then_inc(x_in[b], 16)
            sp.dma_start(w1_sb[:, :], w1).then_inc(q["w1_in"], 16)
            sp.dma_start(w2_sb[:, :, :], w2.rearrange("(c p) d -> p c d", p=P)).then_inc(q["w2_in"], 16)
            sp.dma_start(b1_bc[:, :], b1.partition_broadcast(P)).then_inc(q["bc_in"], 16)
            sp.dma_start(b2_bc[:, :], b2.partition_broadcast(P)).then_inc(q["bc_in"], 16)

            sp.dma_start(vecs[0:NC, :], b1.rearrange("(c p) -> c p", p=P)).then_inc(q["vec_in"], 16)
            for r, vec in enumerate((b2, gamma, beta)):
                sp.dma_start(vecs[NC + r:NC + r + 1, :], vec.rearrange("(a n) -> a n", a=1)).then_inc(q["vec_in"], 16)
            sp.dma_start(wr_sb[:, :], wr).then_inc(q["vec_in"], 16)
            sp.dma_start(br_bc[:, :], br.partition_broadcast(P)).then_inc(q["vec_in"], 16)

            def load_rest():
                for b in range(3, B):
                    sp.dma_start(x_all[:, b], x[b].rearrange("(i p) d -> p i d", p=P)).then_inc(x_in[b], 16)
                sp.wait_ge(q["dve_set"], SETS["rows"])
                sp.dma_start(rows_dram, rows[:, :, :]).then_inc(q["rows_out"], 16)
                sp.wait_ge(q["rows_out"], 16)
                for i in range(ROW_DMAS):
                    bs = slice(i * B // ROW_DMAS, (i + 1) * B // ROW_DMAS)
                    sp.dma_start(rows_bc[:, bs].rearrange("p b r d -> p (b r d)"),
                                 rows_dram[bs].rearrange("b r d -> (b r d)").partition_broadcast(P)).then_inc(rows_in[i], 16)

            def stack(b):
                i = b % 2
                sp.wait_ge(q["split_done"], b + 1)
                sp.dma_start(parts_dram[b, 0:6].rearrange("s p t -> p s t"), part8[:, i]).then_inc(part_w[i], 16)
                sp.dma_start(parts_dram[b, 6:8].rearrange("s p t -> p s t"), part8[:, i, 3:5]).then_inc(part_w[i], 16)
                if b >= ROTS:
                    sp.wait_ge(q["e_done"], 3 * G * (b - ROTS + 1))
                sp.wait_ge(part_w[i], 32 * (b // 2 + 1))
                rowsz = NPART * HD
                for r in range(3):
                    sp.dma_start(Qs[rowsz * r:rowsz * (r + 1), ROT(b)],
                                 parts_dram[b, 0:3].rearrange("s (d h) t -> (s d) h t", d=HD)).then_inc(stack_in[ROT(b)], 16)
                    sp.dma_start(Ks[rowsz * r:rowsz * (r + 1), ROT(b)],
                                 parts_dram[b, 3 + r:6 + r].rearrange("s (d h) t -> (s d) h t", d=HD)).then_inc(stack_in[ROT(b)], 16)

            def mrows(b):
                sp.wait_ge(q["nmlo_done"], b + 1)
                sp.dma_start(Qs[R_S:R_S + 1, ROT(b)], nmT[:, b % 2, 0, :]).then_inc(mrow_in[b % 2], 16)
                sp.dma_start(Qs[R_S + 1:R_E, ROT(b)], nmT[:, b % 2, 1, :]).then_inc(mrow_in[b % 2], 16)

            for t in range(T_END):
                b = batch_at(t, AT_NMT)
                if b is not None:
                    mrows(b)
                b = lo_at(t)
                if b is not None:
                    stack(b)
                    if b == 0:
                        load_rest()
            for p in range(NPAIR - 1):
                sp.wait_ge(q["ob_done"], p + 1)
                sp.dma_start(out[2 * p:2 * p + 2].rearrange("b (i t) d -> t (b i) d", t=P), ob[:, p % 2]).then_inc(stored[p % 2], 16)
            for k in range(2):
                sp.wait_ge(q["ob_done"], NPAIR + k)
                sp.dma_start(out[B - 2 + k].rearrange("(i t) d -> t i d", t=P),
                             ob[:, (NPAIR - 1) % 2, NBLK * k:NBLK * (k + 1)]).then_inc(stored[(NPAIR - 1) % 2], 16)
            sp.wait_ge(stored[0], 16 * 2)
            sp.wait_ge(stored[1], 16 * 3)

        @block.gpsimd
        def _(gp):
            gp.memset(ones_b[:, :], 1.0).then_inc(q["pool_set"], 1)
            gp.memset(mhalf[:, :], -0.5).then_inc(q["pool_set"], 1)
            for i in range(4):
                gp.memset(Vx[:, i], 1.0).then_inc(q["pool_set"], 1)
            gp.memset(beta_w[:, :], 1.0).then_inc(q["pool_set"], 1)
            for col, k in enumerate((K_STAT - 1, P * FF - K_STAT,
                                     2 * (P * FF - K_STAT) - P * FF, 2 * (K_STAT - 1) - P * FF)):
                gp.memset(ktab[:, col:col + 1], float(k)).then_inc(q["pool_set"], 1)

            def rstd(n0, n1_, k):
                gp.wait_ge(q["ln_stat"], k)
                gp.tensor_scalar(ve1[:, n0:n1_], mv1[:, n0:n1_, 1], EPS, None, op0=ALU.add).then_inc(q["pool_self"], 1)
                gp.wait_ge(q["pool_self"], k)
                gp.tensor_tensor(rs1[:, n0:n1_], ve1[:, n0:n1_], mhalf[:, n0:n1_], op=ALU.pow).then_inc(q["ln_rstd"], 1)

            own = [B]

            def deviation(ready, p, ve, mv, rs, done):
                ks = slice(4 * p, 4 * p + 4)
                own[0] += 1
                gp.wait_ge(q[ready], p + 1)
                gp.tensor_scalar(ve[:, ks], mv[:, ks, 1], EPS, None, op0=ALU.add).then_inc(q["pool_self"], 1)
                gp.wait_ge(q["pool_self"], own[0])
                gp.tensor_tensor(rs[:, ks], ve[:, ks], mhalf[:, ks], op=ALU.pow).then_inc(q[done], 1)

            def second_ln(p):
                deviation("ln2_stat", p, ve1, mv1, rs1, "ln2_rstd")

            def router_ln(p):
                deviation("ln3_stat", p, ve3, mv3, rs3, "ln3_rstd")

            def c_exp(p):
                gp.wait_ge(q["logit_done"], p + 1)
                gp.tensor_tensor(ex[:, :, :], eul[:, :, :], lg[:, :, :], op=ALU.pow).then_inc(q["ex_done"], 1)

            gp.memset(eul[:, :, :], math.e).then_inc(q["pool_set"], 1)
            gp.wait_ge(q["pool_set"], POOL_SETS)
            rstd(0, NBLK, 1)
            def rot(a):
                return a.rearrange("r (h t) -> r h t", h=NH).unsqueeze(1).broadcast_to([a.shape[0], ROTS, NH, S])
            gp.dma_start(Qs[R_PROD:R_S], rot(q_const)).then_inc(q["const_in"], 16)
            gp.dma_start(Ks[R_PROD:R_E], rot(k_const)).then_inc(q["const_in"], 16)
            gp.dma_start(mask5[:, :, :], mask_c.rearrange("p (h k) -> p h k", h=HG + 1)).then_inc(q["const_in"], 16)
            for t in range(T_END):
                if sel_bit(t) is not None:
                    n = sel_bit(t)
                    gp.wait_ge(q["cand_done"], n + 1)
                    if n:
                        gp.wait_ge(q["cnt_done"], n)
                    gp.tensor_scalar(msk[:, 1], w2a[:, :], cand[:, 1:2].bitcast(F32), None, op0=ALU.is_lt).then_inc(q["m_pool"], 1)
                k = (t - B1_STEP) // 2
                if (t - B1_STEP) % 2 == 0 and 0 <= k < 2 * NC:
                    gp.wait_ge(q["b1abs_done"], 1)
                    gp.tensor_scalar(rmask[:, k % 2, k // 2], b1a[:, :], colsa[:, k // 2:k // 2 + 1], None,
                                     op0=(ALU.is_gt, ALU.is_lt)[k % 2]).then_inc(q["b1m_done"], 1)
                b = batch_at(t, AT_QK)
                if b is not None and b + 1 < B:
                    rstd(NBLK * (b + 1), NBLK * (b + 2), b + 2)
                b, g, e = lagged(t, E_LAG)
                if b is not None:
                    for j in range(3):
                        gp.wait_ge(q["exp_done"], 3 * e + j + 1)
                        if j == 0:
                            v = PT[:, e % 2, 0].rearrange("p (h q) -> p h q", h=HG)
                        else:
                            v = PT[:, e % 2, j].rearrange("p (h q) -> p h q", h=2)[:, :, 0:P]
                        gp.affine_select(out=v, in_=v, compare_op=ALU.is_ge, fill=0.0, base=0,
                                         pattern=[[0, v.shape[1]], [1, P]], channel_multiplier=-1).then_inc(q["sel_done"], 1)
                if t in LN_STAT_AT:
                    second_ln(LN_STAT_AT[t])
                if t - 1 in LN_NEXT_AT:
                    router_ln(LN_NEXT_AT[t - 1])
                if t == FFN_STEP:
                    c_exp(0)
            second_ln(NPAIR - 1)
            router_ln(NPAIR - 1)
            for p in range(1, NPAIR):
                c_exp(p)

        @block.scalar
        def _(act):
            act.dma_start(ident[:, :], ident_c).then_inc(q["ident_in"], 16)
            act.dma_start(wqkv_in[:, :, :], w_qkv.rearrange("(j p) d -> p j d", p=P)).then_inc(q["qkvw_in"], 16)
            act.dma_start(wo_in[:, :], w_o).then_inc(q["qkvw_in"], 16)
            act.wait_ge(q["pe_set"], 1)
            act.activation(c_e[:, :], psQ[:, 0:B], ACT.Exp, scale=-1.0).then_inc(q["act_set"], 1)

            def exp_unit(t, j):
                b, g, e = lagged(t, E_LAG)
                if b is None:
                    return
                u = 3 * e + j
                act.wait_ge(q["e_done"], u + 1)
                if e >= 2 and j == 0:
                    act.wait_ge(q["pv_done"], e - 1)
                act.activation(PT[:, e % 2, j], psE[u % 2][:, :], ACT.Exp).then_inc(q["exp_done"], 1)

            def sign_mask(n, col, w):
                if n is None:
                    return
                act.wait_ge(q["cand_done"], n + 1)
                if n:
                    act.wait_ge(q["cnt_done"], n)
                act.activation(msk[:, col], w[:, :], ACT.Sign, bias=cand[:, col:col + 1].bitcast(F32),
                               scale=-(1.0 - 2.0 ** -24)).then_inc(q["m_act"], 1)

            def c_act_h(p):
                act.wait_ge(q["h2T_psum"], p + 1)
                if p >= 2:
                    act.wait_ge(q["f1_done"], 4 * 2 * (p - 1))
                    act.wait_ge(q["lgT_done"], p - 1)
                act.activation(h2T[:, p % 2], (psE[1] if p else psX)[:, :], ACT.Copy).then_inc(q["h2T_done"], 1)

            def c_act_l(p):
                act.wait_ge(q["lgT_done"], p + 1)
                if p:
                    act.wait_ge(q["lg_psum"], p)
                act.activation(lgT[:, :], (psE[1] if p else psX)[0:NE, :], ACT.Copy).then_inc(q["lgT_out"], 1)

            def gelus(n):
                p, w = n // 2, n % 2
                for ch in range(NC):
                    act.wait_ge(q["f1_done"], 4 * n + ch + 1)
                    if n >= 2 and ch == 0:
                        act.wait_ge(q["f2_done"], n - 1)
                    if n == 1 and ch == 0:
                        act.wait_ge(q["b1p_done"], 1)
                    bias = b1p[:, ch:ch + 1] if w else cols[:, ch:ch + 1]
                    act.activation(hid[:, n % 2, ch, :], psF[(4 * n + ch) % NF][:, :], ACT.Gelu_apprx_tanh,
                                   bias=bias).then_inc(q["gelu_done"], 1)

            for t in range(T_END):
                n = sel_bit(t)
                if n == 0:
                    act.wait_ge(q["w1_in"], 16)
                    act.activation(w1a[:, :], w1_sb[:, :], ACT.Abs).then_inc(q["act_set"], 1)
                    act.wait_ge(q["w2_in"], 16)
                    act.activation(w2a[:, :], w2_sb.rearrange("p c d -> p (c d)"), ACT.Abs).then_inc(q["act_set"], 1)
                sign_mask(n, 2, w1a)
                b = batch_at(t, AT_NMT)
                if b is not None:
                    act.wait_ge(q["nmT_done"], b + 1)
                    if b >= 2:
                        act.wait_ge(mrow_in[b % 2], 32 * (b // 2))
                    act.activation(nmT[:, b % 2, 0, :], psX[0:NH, 0:S], ACT.Copy).then_inc(q["nmhi_done"], 1)
                b = batch_at(t, AT_OT)
                if b is not None:
                    act.wait_ge(q["at_done"], b + 1)
                    if b:
                        act.wait_ge(q["y_done"], b)
                    act.activation(AT[:, :], psX[:, 0:S], ACT.Copy).then_inc(q["at_out"], 1)
                b = batch_at(t, AT_V)
                if b is not None:
                    act.wait_ge(q["v_done"], b + 1)
                    if b == 0:
                        act.wait_ge(q["pool_set"], POOL_SETS)
                    if b >= 4:
                        act.wait_ge(q["pv_done"], G * (b - 3))
                    act.activation(Vx[:, b % 4, :, :, 0:HD],
                                   psX[:, 0:S].rearrange("p (i h d) -> p i h d", i=NBLK, h=NH),
                                   ACT.Copy).then_inc(q["v_out"], 1)
                sign_mask(n, 3, w2a)
                exp_unit(t, 0)
                exp_unit(t, 1)
                b, g, e = lagged(t, E_LAG + 1)
                if b is not None:
                    act.wait_ge(q["pv_done"], e + 1)
                    if e >= 2:
                        act.wait_ge(q["ut_done"], e - 1)
                    act.activation(U[:, e % 2], psO[:, 0:S], ACT.Copy).then_inc(q["u_done"], 1)
                exp_unit(t, 2)
                b = batch_at(t, AT_T)
                if b is not None:
                    act.wait_ge(q["t_done"], b + 1)
                    if b >= 2:
                        act.wait_ge(q["v_done"], b - 1)
                    if b == 0:
                        act.wait_ge(q["dve_set"], SETS["modT"])
                    act.activation(h1T[:, b % 2], psQ[:, 0:S], ACT.Identity, scale=modT[:, 1, b:b + 1],
                                   bias=modT[:, 0, b:b + 1]).then_inc(q["h1_done"], 1)
                b = batch_at(t, AT_QK)
                if b is not None:
                    act.wait_ge(q["qk_done"], b + 1)
                    if b >= 2:
                        act.wait_ge(part_w[b % 2], 32 * (b // 2))
                    act.activation(part8[:, b % 2, 0:4:3, :], psQ.rearrange("p (a t) -> p a t", a=2),
                                   ACT.Copy).then_inc(q["hi_done"], 1)
                if t == FIRST_STEP:
                    c_act_h(0)
                if t == FIRST_STEP + 1:
                    c_act_l(0)
                if t == FFN_STEP:
                    gelus(0)

            for n in range(1, 2 * NPAIR):
                gelus(n)
                if n % 2 and n // 2 + 1 < NPAIR:
                    c_act_h(n // 2 + 1)
                    c_act_l(n // 2 + 1)

        @block.tensor
        def _(pe):
            mm = nc.tensor.matmul
            tr = nc.tensor.transpose
            pe.wait_ge(q["c_in"], 16)
            pe.wait_ge(q["ident_in"], 16)
            tr(psQ[:, 0:B], c_in[:, :], ident[0:B, 0:B]).then_inc(q["pe_set"], 1)
            pe.wait_ge(q["qkvw_in"], 32)
            for j in range(3):
                tr(psS[0][:, j * P:(j + 1) * P], wqkv_in[:, j, :], ident[:, :])
            tr(psS[0][:, 3 * P:4 * P], wo_in[:, :], ident[:, :]).then_inc(q["pe_set"], 1)
            pe.wait_ge(q["dve_set"], SETS["silu"])
            pe.wait_ge(q["wmod_in"], 16)
            for j in range(2):
                last = mm(psE[0][:, j * B:(j + 1) * B], wmod_sb[:, j * D:(j + 1) * D], c_s[:, :], start=True, stop=True)
            last.then_inc(q["pe_set"], 1)
            mm(psE[1][0:B, 0:512], c_s[:, :], wmod_sb[:, 2 * D:6 * D], start=True, stop=True).then_inc(q["pe_set"], 1)

            def vectors():
                pe.wait_ge(q["vec_in"], 16 * 6)
                tr(psS[1][:, 0:NC + 3], vecs[:, :], ident[0:NC + 3, 0:NC + 3]).then_inc(q["pe_set"], 1)

            def router_sums():
                pe.wait_ge(q["pool_set"], POOL_SETS)
                pe.wait_ge(q["dve_set"], SETS["beta"])
                mm(psO[:, 0:NE], beta_w[:, :], wrg[:, :], start=True, stop=True)
                mm(psO[:, NE:2 * NE], woTg[:, 0, :], wr_sb[:, :], start=True, stop=True).then_inc(q["pe_set"], 1)

            def s_unit(t, j):
                b, g, m = lagged(t, M_LAG)
                if b is None:
                    return
                u, r, bank = 3 * m + j, ROT(b), psS[(3 * m + j) % 2]
                if m == 0 and j == 0:
                    pe.wait_ge(q["const_in"], 16 * 3)
                    pe.wait_ge(q["dve_set"], SETS["all"])
                if g == 0 and j == 0:
                    pe.wait_ge(stack_in[r], 96 * (b // ROTS + 1))
                if u >= 2:
                    pe.wait_ge(q["max_done"], u - 1)
                if j == 0:
                    mm(bank[:, :], mask5[:, HG, :], mask5[:, 0:HG, :].rearrange("p h k -> p (h k)"), start=True, stop=False, skip_group_check=True)
                    for i in range(HG):
                        h = HG * g + i
                        last = mm(bank[:, i * P:(i + 1) * P], Qs[0:R_S, r, h, 0:P], Ks[0:R_S, r, h, 0:P],
                                  start=False, stop=True, skip_group_check=True)
                else:
                    mm(bank.rearrange("p (h k) -> p h k", h=2)[:, :, P:S], mask5[:, HG, :], mask5[:, 0:2, :],
                       start=True, stop=False, skip_group_check=True)
                    for i in range(2):
                        h = HG * g + 2 * (j - 1) + i
                        last = mm(bank[:, i * S:(i + 1) * S], Qs[0:R_S, r, h, P:S], Ks[0:R_S, r, h, :],
                                  start=False, stop=True, skip_group_check=True)
                last.then_inc(q["s_done"], 1)

            def e_unit(t, j):
                b, g, e = lagged(t, E_LAG)
                if b is None:
                    return
                u, r, bank = 3 * e + j, ROT(b), psE[(3 * e + j) % 2]
                if g == 0 and j == 0:
                    pe.wait_ge(mrow_in[b % 2], 32 * (b // 2 + 1))
                if u >= 2:
                    pe.wait_ge(q["exp_done"], u - 1)
                if j == 0:
                    for i in range(HG):
                        h = HG * g + i
                        last = mm(bank[:, i * P:(i + 1) * P], Ks[0:R_E, r, h, P:S], Qs[0:R_E, r, h, P:S],
                                  start=True, stop=True, skip_group_check=True)
                else:
                    for i in range(2):
                        h = HG * g + 2 * (j - 1) + i
                        last = mm(bank[:, i * S:(i + 1) * S], Ks[0:R_E, r, h, 0:P], Qs[0:R_E, r, h, :],
                                  start=True, stop=True, skip_group_check=True)
                last.then_inc(q["e_done"], 1)

            def pv(t):
                b, g, e = lagged(t, E_LAG + 1)
                if b is None:
                    return
                pe.wait_ge(q["sel_done"], 3 * e + 3)
                if g == 0:
                    pe.wait_ge(q["v_out"], b + 1)
                if e:
                    pe.wait_ge(q["u_done"], e)
                pt0 = PT[:, e % 2, 0].rearrange("p (h q) -> p h q", h=HG)
                for i in range(HG):
                    h = HG * g + i
                    mm(psO[32 * i:32 * i + 32, 0:S], Vx[:, b % 4, 0, h, :],
                       PT[:, e % 2, 1 + i // 2, (i % 2) * S:(i % 2 + 1) * S], start=True, stop=False,
                       skip_group_check=True)
                for i in range(HG):
                    h = HG * g + i
                    last = mm(psO[32 * i:32 * i + 32, P:S], Vx[:, b % 4, 1, h, :], pt0[:, i, :],
                              start=False, stop=True, skip_group_check=True)
                last.then_inc(q["pv_done"], 1)

            def ut(t):
                b, g, e = lagged(t, E_LAG + 1)
                if b is None:
                    return
                pe.wait_ge(q["u_done"], e + 1)
                if e:
                    pe.wait_ge(q["a_done"], e)
                for i in range(NBLK):
                    last = tr(psU[:, i * P:(i + 1) * P], U[:, e % 2, i * P:(i + 1) * P], ident[:, :])
                last.then_inc(q["ut_done"], 1)

            free_x = [None]

            def claim_x(reader):
                if free_x[0]:
                    pe.wait_ge(*free_x[0])
                free_x[0] = reader

            def c_pe_h(p):
                pe.wait_ge(q["h2_done"], p + 1)
                if p == 0:
                    claim_x((q["h2T_done"], 1))
                elif p > 1:
                    pe.wait_ge(q["lgT_out"], p)
                for i in range(4):
                    last = tr((psE[1] if p else psX)[:, i * P:(i + 1) * P], h2[:, p, i, :], ident[:, :])
                last.then_inc(q["h2T_psum"], 1)

            def c_pe_l(p):
                pe.wait_ge(q["h2T_done"], p + 1)
                if p == 0:
                    claim_x((q["lgT_out"], 1))
                mm((psE[1] if p else psX)[0:NE, :], wrg[:, :], h2T[:, p % 2], start=True, stop=True).then_inc(q["lgT_done"], 1)

            def c_pe_t(p):
                pe.wait_ge(q["lgT_out"], p + 1)
                claim_x((q["lg_read"], p + 1))
                for i in range(4):
                    last = tr(psX[:, i * NE:(i + 1) * NE], lgT[:, i * P:(i + 1) * P], ident[0:NE, 0:NE])
                last.then_inc(q["lg_psum"], 1)

            def f1(n, chunks=range(NC)):
                p, w = n // 2, n % 2
                wt = w1p if w else w1_sb
                if w == 0:
                    pe.wait_ge(q["h2T_done"], p + 1)
                if n == 1:
                    pe.wait_ge(q["pert_done"], 1)
                for ch in chunks:
                    k = NC * n + ch
                    if k < 2:
                        pe.wait_ge(q["max_done"], 3 * G * B)
                    elif k == 2:
                        pe.wait_ge(q["res_done"], B)
                    elif k == 3:
                        pe.wait_ge(q["exp_done"], 3 * G * B)
                    else:
                        pe.wait_ge(q["gelu_done"], k - NF + 1)
                    mm(psF[k % NF][:, :], wt[:, ch * P:(ch + 1) * P], h2T[:, p % 2], start=True, stop=True).then_inc(q["f1_done"], 1)

            def f2(n):
                p, w = n // 2, n % 2
                wt, bank = (w2p, psU) if w else (w2_sb, psO)
                if p:
                    pe.wait_ge(q["y_read"], n - 1)
                if n == 1:
                    pe.wait_ge(q["pert_done"], 2)
                pe.wait_ge(q["gelu_done"], 4 * (n + 1))
                for i in range(4):
                    if n == 2 * NPAIR - 1 and i == 2:
                        last.then_inc(q["f2_done"], 1)
                        claim_x(None)
                        bank = psX
                    for ch in range(NC):
                        last = mm(bank[:, i * P:(i + 1) * P], hid[:, n % 2, ch, i * P:(i + 1) * P], wt[:, ch, :],
                                  start=(ch == 0), stop=(ch == NC - 1), skip_group_check=True)
                last.then_inc(q["f2_done"], 1)

            def count(n):
                if n is None:
                    return
                claim_x((q["cnt_out"], n + 1))
                pe.wait_ge(q["m_dve"], n + 1)
                pe.wait_ge(q["m_act"], 2 * n + 2)
                pe.wait_ge(q["m_pool"], n + 1)
                for col in range(4):
                    for ch in range(NC):
                        last = mm(psX[:, col * NC + ch:col * NC + ch + 1], msk[:, col, ch * P:(ch + 1) * P],
                                  ones_b[:, 0:1], start=True, stop=True, skip_group_check=True)
                last.then_inc(q["cnt_done"], 1)

            def total(n):
                if n is None:
                    return
                claim_x((q["cond_done"], n + 1))
                for ch in range(NC):
                    last = mm(psX[:, 0:4], ones_b[:, :], cnt[:, :, ch], start=(ch == 0), stop=(ch == NC - 1))
                last.then_inc(q["tot_done"], 1)

            for t in range(T_END):
                n = sel_bit(t)
                if t == B1_USE:
                    pe.wait_ge(q["b1m_done"], 2 * NC)
                    claim_x((q["b1p_done"], 1))
                    for k in range(2):
                        for ch in range(NC):
                            for j in range(NC):
                                last = mm(psX[:, k * NC + ch:k * NC + ch + 1], rmask[:, k, j, ch * P:(ch + 1) * P], ones_b[:, 0:1],
                                          start=(j == 0), stop=(j == NC - 1), skip_group_check=True)
                    last.then_inc(q["b1rank"], 1)
                if t == B2_USE:
                    pe.wait_ge(q["b2m_done"], 1)
                    claim_x((q["b2p_done"], 1))
                    mm(psX[:, 0:2 * P], ones_b[:, :], b2m.rearrange("p a d -> p (a d)"), start=True, stop=True).then_inc(q["b2rank"], 1)
                b = batch_at(t, AT_NMT)
                if b is not None:
                    pe.wait_ge(q["max_done"], 3 * G * (b + 1))
                    claim_x((q["nmlo_done"], b + 1))
                    for i in range(NBLK):
                        last = tr(psX[0:NH, i * P:(i + 1) * P], nmax[:, b % 2, i, :], ident[:, :])
                    last.then_inc(q["nmT_done"], 1)
                b = batch_at(t, AT_V)
                if b is not None:
                    claim_x((q["v_out"], b + 1))
                    for i in range(NBLK):
                        last = mm(psX[:, i * P:(i + 1) * P], h1T[:, b % 2, i * P:(i + 1) * P], wvT[:, :], start=True, stop=True)
                    last.then_inc(q["v_done"], 1)
                b = batch_at(t, AT_Y)
                if b is not None:
                    pe.wait_ge(q["wog_done"], b + 1)
                    claim_x((q["x2_done"], b + 1))
                    for i in range(NBLK):
                        last = mm(psX[:, i * P:(i + 1) * P], AT[:, i * P:(i + 1) * P], woTg[:, b, :], start=True, stop=True)
                    last.then_inc(q["y_done"], 1)
                s_unit(t, 0)
                e_unit(t, 0)
                s_unit(t, 1)
                e_unit(t, 1)
                b = batch_at(t, AT_OT)
                if b is not None:
                    pe.wait_ge(q["a_done"], G * (b + 1))
                    claim_x((q["at_out"], b + 1))
                    for i in range(NBLK):
                        last = tr(psX[:, i * P:(i + 1) * P], A[:, b % 2, i, :], ident[:, :])
                    last.then_inc(q["at_done"], 1)
                pv(t)
                count(n)
                s_unit(t, 2)
                total(n)
                e_unit(t, 2)
                ut(t)
                b = batch_at(t, AT_T)
                if b is not None:
                    pe.wait_ge(q["n1_done"], b + 1)
                    if b == 0:
                        pe.wait_ge(q["dve_set"], SETS["silu"])
                    else:
                        pe.wait_ge(q["res_done"], b)
                    for i in range(NBLK):
                        last = tr(psQ[:, i * P:(i + 1) * P], n1[:, b % 2, i, :], ident[:, :])
                    last.then_inc(q["t_done"], 1)
                b = batch_at(t, AT_QK)
                if b is not None:
                    pe.wait_ge(q["h1_done"], b + 1)
                    for a in range(2):
                        last = mm(psQ[:, a * S:(a + 1) * S], wqkT[:, a, :], h1T[:, b % 2], start=True, stop=True)
                    last.then_inc(q["qk_done"], 1)
                if t == VEC_STEP - 1:
                    vectors()
                if t == VEC_STEP:
                    router_sums()
                if t == FIRST_STEP:
                    c_pe_h(0)
                if t == FIRST_STEP + 1:
                    c_pe_l(0)
                if 0 < t - FIRST_STEP < NC:
                    f1(0, (t - FIRST_STEP - 1,))
                if t == FFN_STEP - 1:
                    c_pe_t(0)
                if t == FFN_STEP:
                    f1(0, (NC - 1,))
                    f1(1, range(NC // 2))
                if t > FFN_STEP:
                    f1(1, (NC // 2 + t - FFN_STEP - 1,))
            for n in range(1, 2 * NPAIR + 1):
                if 1 < n < 2 * NPAIR:
                    f1(n)
                if n % 2 == 0 and n // 2 < NPAIR:
                    c_pe_t(n // 2)
                if n % 2 and (n + 1) // 2 < NPAIR:
                    c_pe_h((n + 1) // 2)
                f2(n - 1)
                if n % 2 and (n + 1) // 2 < NPAIR:
                    c_pe_l((n + 1) // 2)

        @block.vector
        def _(v):
            ve = nc.vector
            own = [0]

            def then_self(inst):
                own[0] += 1
                inst.then_inc(q["dve_self"], 1)
                v.wait_ge(q["dve_self"], own[0])

            def absolute(dst, src):
                return ve.tensor_scalar(dst.bitcast(U32), src.bitcast(U32), 0x7FFFFFFF, None, op0=ALU.bitwise_and)

            def ln1(b):
                v.wait_ge(x_in[b], 16)
                for i in range(NBLK):
                    last = ve.bn_stats(st1[:, 2 * b + i, :], x_all[:, b, i, :])
                then_self(last)
                for i in range(NBLK):
                    last = ve.bn_aggr(mv1[:, 2 * b + i, :], st1[:, 2 * b + i, :])
                last.then_inc(q["ln_stat"], 1)

            ln1(0)
            ds = lambda inst: inst.then_inc(q["dve_set"], 1)
            v.wait_ge(q["act_set"], 1)
            ds(ve.tensor_scalar(c_e[:, :], c_e[:, :], 1.0, None, op0=ALU.add))
            v.wait_ge(q["dve_set"], SETS["sil1"])
            ds(ve.reciprocal(c_e[:, :], c_e[:, :]))
            v.wait_ge(q["dve_set"], SETS["sil2"])
            ds(ve.tensor_tensor(c_s[:, :], psQ[:, 0:B], c_e[:, :], op=ALU.mult))
            v.wait_ge(q["pe_set"], 2)
            ds(ve.tensor_scalar(wqkT[:, 0, :].rearrange("p (d h) -> p h d", d=HD),
                                psS[0][:, 0:P].rearrange("p (h d) -> p h d", h=NH), float(HD) ** -0.5, None, op0=ALU.mult))
            ds(ve.tensor_copy(wqkT[:, 1, :].rearrange("p (d h) -> p h d", d=HD),
                              psS[0][:, P:2 * P].rearrange("p (h d) -> p h d", h=NH)))
            ds(ve.tensor_copy(wvT[:, :], psS[0][:, 2 * P:3 * P]))
            ds(ve.tensor_copy(woT[:, :], psS[0][:, 3 * P:4 * P]))
            v.wait_ge(q["pe_set"], 3)
            ds(ve.tensor_copy(modT[:, 0, :], psE[0][:, 0:B]))
            ds(ve.tensor_scalar(modT[:, 1, :], psE[0][:, B:2 * B], 1.0, None, op0=ALU.add))

            def make_rows():
                v.wait_ge(q["pe_set"], 4)
                pg = psE[1][0:B, :].rearrange("b (r d) -> b r d", r=4)
                ds(absolute(rows[:, 0:2, :], pg[:, 0:4:3, :]))
                v.wait_ge(q["dve_set"], SETS["absg"])
                ds(ve.tensor_scalar(rows[:, 0:2, :], rows[:, 0:2, :], 0.25, None, op0=ALU.max))
                ds(ve.tensor_scalar(rowt[:, :, :], pg[:, 0:4:3, :], 0.0, 2.0, op0=ALU.is_ge, op1=ALU.mult))
                v.wait_ge(q["dve_set"], SETS["sgn"])
                ds(ve.tensor_scalar(rowt[:, :, :], rowt[:, :, :], -1.0, None, op0=ALU.add))
                v.wait_ge(q["dve_set"], SETS["sgn2"])
                ds(ve.tensor_tensor(rows[:, 0:2, :], rows[:, 0:2, :], rowt[:, :, :], op=ALU.mult))
                ds(ve.tensor_scalar(rows[:, 2, :], pg[:, 2, :], 1.0, None, op0=ALU.add))
                ds(ve.tensor_copy(rows[:, 3, :], pg[:, 1, :]))

            def vector_columns():
                v.wait_ge(q["pe_set"], 5)
                ds(ve.tensor_copy(cols[:, :], psS[1][:, 0:NC + 3]))
                v.wait_ge(q["dve_set"], SETS["cols"])
                ds(ve.tensor_scalar(wrg[:, :], wr_sb[:, :], cols[:, NC + 1:NC + 2], None, op0=ALU.mult))
                ds(ve.tensor_copy(woTg[:, 0, :], cols[:, NC + 2:NC + 3].broadcast_to([P, P])))

            def router_constants():
                v.wait_ge(q["pe_set"], 6)
                ds(ve.tensor_copy(gsum[:, 0:NE], psO[:, 0:NE]))
                ds(ve.tensor_tensor(gsum[:, NE:2 * NE], psO[:, NE:2 * NE], br_bc[:, :], op=ALU.add))
                v.wait_ge(q["pool_set"], POOL_SETS)

            def or_next(dst, n):
                bit = 1 << (NBITS - 1 - n)
                ve.tensor_scalar(dst[:, 0:2], cur[:, 0:2], bit, None, op0=ALU.bitwise_or)
                return ve.tensor_scalar(dst[:, 2:4], cur[:, 2:4], bit - 1, None, op0=ALU.bitwise_or)

            def first_cand():
                then_self(ve.memset(cur[:, :], 0))
                v.wait_ge(q["act_set"], 3)
                then_self(or_next(cand, 0))
                or_next(nxt, 1).then_inc(q["cand_done"], 1)

            def dve_mask(n):
                v.wait_ge(q["cand_done"], n + 1)
                ve.tensor_scalar(msk[:, 0], w1a[:, :], cand[:, 0:1].bitcast(F32), None, op0=ALU.is_lt).then_inc(q["m_dve"], 1)

            def settle(n, between):
                bit = NBITS - 1 - n
                v.wait_ge(q["tot_done"], n + 1)
                ve.tensor_tensor(cond[:, :], psX[:, 0:4], ktab[:, :], op=ALU.is_le).then_inc(q["cond_done"], 1)
                between()
                v.wait_ge(q["cond_done"], n + 1)
                if bit:
                    if n:
                        v.wait_ge(q["nxt_done"], n)
                    ve.scalar_tensor_tensor(cand[:, :], cond[:, :], bit, nxt[:, :], op0=ALU.logical_shift_left,
                                            op1=ALU.bitwise_or).then_inc(q["cand_done"], 1)
                ve.scalar_tensor_tensor(cur[:, :], cond[:, :], bit, cur[:, :], op0=ALU.logical_shift_left,
                                        op1=ALU.bitwise_or).then_inc(q["cur_done"], 1)
                if bit:
                    dve_mask(n + 1)
                if bit > 1:
                    v.wait_ge(q["cur_done"], n + 1)
                    or_next(nxt, n + 2).then_inc(q["nxt_done"], 1)

            def maxima(t, j):
                b, g, m = lagged(t, M_LAG)
                if b is None:
                    return
                if g == 0 and j == 0 and b >= 2:
                    v.wait_ge(q["nmT_done"], b - 1)
                v.wait_ge(q["s_done"], 3 * m + j + 1)
                bank = psS[(3 * m + j) % 2]
                if j == 0:
                    ve.tensor_reduce(nmax[:, b % 2, 0, HG * g:HG * (g + 1)], bank.rearrange("p (h k) -> p h k", h=HG),
                                     axis=AX.X, op=ALU.max, negate=True).then_inc(q["max_done"], 1)
                else:
                    h = HG * g + 2 * (j - 1)
                    ve.tensor_reduce(nmax[:, b % 2, 1, h:h + 2], bank.rearrange("p (h k) -> p h k", h=2),
                                     axis=AX.X, op=ALU.max, negate=True).then_inc(q["max_done"], 1)

            def second_stats(p):
                xp = x_all[:, 2 * p:2 * p + 2].rearrange("p b i d -> p (b i) d")
                v.wait_ge(q["x2_done"], 2 * p + 2)
                for i in range(4):
                    last = ve.bn_stats(st1[:, 4 * p + i, :], xp[:, i, :])
                then_self(last)
                for i in range(4):
                    last = ve.bn_aggr(mv1[:, 4 * p + i, :], st1[:, 4 * p + i, :])
                last.then_inc(q["ln2_stat"], 1)

            def second_use(p):
                xp = x_all[:, 2 * p:2 * p + 2].rearrange("p b i d -> p (b i) d")
                v.wait_ge(q["ln2_rstd"], p + 1)
                for i in range(4):
                    k = 4 * p + i
                    last = ve.tensor_scalar(n2[:, i, :], xp[:, i, :], mv1[:, k, 0:1], rs1[:, k:k + 1],
                                            op0=ALU.subtract, op1=ALU.mult)
                then_self(last)
                for i in range(ROW_DMAS):
                    v.wait_ge(rows_in[i], 16)
                for r, src in ((2, n2), (3, h2[:, p])):
                    for k in range(2):
                        ks = slice(2 * k, 2 * k + 2)
                        last = ve.tensor_tensor(h2[:, p, ks, :], src[:, ks, :],
                                                rows_bc[:, 2 * p + k, r, :].unsqueeze(1).broadcast_to([P, NBLK, D]),
                                                op=ALU.mult if r == 2 else ALU.add)
                    if r == 2:
                        then_self(last)
                last.then_inc(q["h2_done"], 1)

            def router_stats(p):
                v.wait_ge(q["h2_done"], p + 1)
                for i in range(4):
                    last = ve.bn_stats(st1[:, 4 * p + i, :], h2[:, p, i, :])
                then_self(last)
                for i in range(4):
                    last = ve.bn_aggr(mv3[:, 4 * p + i, :], st1[:, 4 * p + i, :])
                last.then_inc(q["ln3_stat"], 1)

            def router_logits(p):
                ks = slice(4 * p, 4 * p + 4)
                e8 = lambda a: a.unsqueeze(2).broadcast_to([P, 4, NE])
                g8 = lambda a: a.unsqueeze(1).broadcast_to([P, 4, NE])
                v.wait_ge(q["ln3_stat"], p + 1)
                then_self(ve.tensor_tensor(lt[:, :, :], e8(mv3[:, ks, 0]), g8(gsum[:, 0:NE]), op=ALU.mult))
                v.wait_ge(q["lg_psum"], p + 1)
                ve.tensor_tensor(lg[:, :, :], psX[:, 0:4 * NE].rearrange("p (i e) -> p i e", i=4), lt[:, :, :],
                                 op=ALU.subtract).then_inc(q["lg_read"], 1)
                v.wait_ge(q["lg_read"], p + 1)
                v.wait_ge(q["ln3_rstd"], p + 1)
                then_self(ve.tensor_tensor(lg[:, :, :], lg[:, :, :], e8(rs3[:, ks]), op=ALU.mult))
                then_self(ve.tensor_tensor(lg[:, :, :], lg[:, :, :], g8(gsum[:, NE:2 * NE]), op=ALU.add))
                then_self(ve.tensor_reduce(lmax[:, :], lg[:, :, :], axis=AX.X, op=ALU.max))
                ve.tensor_tensor(lg[:, :, :], lg[:, :, :], e8(lmax[:, :]), op=ALU.subtract).then_inc(q["logit_done"], 1)

            def router_weights(p):
                v.wait_ge(q["ex_done"], p + 1)
                ve.tensor_reduce(esum[:, :], ex[:, :, :], axis=AX.X, op=ALU.add)
                then_self(ve.tensor_reduce(esum1[:, :], ex[:, :, 1:NE], axis=AX.X, op=ALU.add))
                then_self(ve.reciprocal(esum[:, :], esum[:, :]))
                ve.tensor_tensor(pr[:, p % 2, 0, :], ex[:, :, 0], esum[:, :], op=ALU.mult)
                then_self(ve.tensor_tensor(pr[:, p % 2, 1, :], esum1[:, :], esum[:, :], op=ALU.mult))
                if p:
                    v.wait_ge(q["ob_done"], p)
                for w in range(2):
                    last = ve.tensor_tensor(yt[:, w], (b2p_bc if w else b2_bc)[:, :].unsqueeze(1).broadcast_to([P, 4, D]),
                                            pr[:, p % 2, w, :].unsqueeze(2).broadcast_to([P, 4, D]), op=ALU.mult)
                then_self(last)
                then_self(ve.tensor_tensor(yt[:, 1], yt[:, 1], yt[:, 0], op=ALU.add))

            def combine(n):
                p, w = n // 2, n % 2
                if w == 0:
                    pieces = ((psO, range(4)),)
                elif p < NPAIR - 1:
                    pieces = ((psU, range(4)),)
                else:
                    pieces = ((psU, range(2)), (psX, range(2, 4)))
                for k, (bank, blocks) in enumerate(pieces):
                    bs = slice(blocks[0], blocks[-1] + 1)
                    v.wait_ge(q["f2_done"], n + 1 + k)
                    for i in blocks:
                        last = ve.scalar_tensor_tensor(yt[:, w, i], bank[:, i * P:(i + 1) * P], pr[:, p % 2, w, i:i + 1],
                                                       yt[:, 1 - w, i], op0=ALU.mult, op1=ALU.add)
                    last.then_inc(q["y_read"], 1)
                    v.wait_ge(q["y_read"], n + 1 + k)
                    if w:
                        for i in blocks[::NBLK]:
                            b = 2 * p + i // NBLK
                            last = ve.tensor_tensor(yt[:, 1, i:i + NBLK], yt[:, 1, i:i + NBLK],
                                                    rows_bc[:, b, 1, :].unsqueeze(1).broadcast_to([P, NBLK, D]), op=ALU.mult)
                        if p >= 2 and k == 0:
                            v.wait_ge(stored[p % 2], 16 * (p // 2))
                        then_self(last)
                        xp = x_all[:, 2 * p:2 * p + 2].rearrange("p b i d -> p (b i) d")
                        ve.tensor_tensor(ob[:, p % 2, bs], yt[:, 1, bs], xp[:, bs], op=ALU.add).then_inc(q["ob_done"], 1)

            def find_tiers(a, top, bot):
                t0, t1 = msk[:, 0], msk[:, 1]
                then_self(ve.tensor_scalar(t0, a, top.bitcast(F32), None, op0=ALU.is_ge))
                then_self(ve.scalar_tensor_tensor(t1, a, bot.bitcast(F32), t0, op0=ALU.is_le, op1=ALU.is_gt))
                then_self(ve.tensor_tensor(t1, t1, t0, op=ALU.subtract))

            def perturb(w, dst):
                then_self(ve.scalar_tensor_tensor(dst, w, 0.8, msk[:, 1], op0=ALU.mult, op1=ALU.mult))
                ve.tensor_tensor(dst, dst, w, op=ALU.add).then_inc(q["pert_done"], 1)

            def tiers(low, high, w, dst, tmp, k, done):
                then_self(ve.tensor_scalar(tmp, high, float(k - 1), None, op0=ALU.is_le))
                then_self(ve.scalar_tensor_tensor(dst, low, float(k - 1), tmp, op0=ALU.is_le, op1=ALU.is_gt))
                then_self(ve.tensor_tensor(dst, dst, tmp, op=ALU.subtract))
                then_self(ve.scalar_tensor_tensor(dst, w, 0.8, dst, op0=ALU.mult, op1=ALU.mult))
                ve.tensor_tensor(dst, dst, w, op=ALU.add).then_inc(q[done], 1)

            def bias_sizes():
                v.wait_ge(q["bc_in"], 32)
                absolute(colsa[:, :], cols[:, :])
                absolute(b1a[:, :], b1_bc[:, :]).then_inc(q["b1abs_done"], 1)

            def perturb_b1():
                v.wait_ge(q["b1rank"], 1)
                tiers(psX[:, 0:NC], psX[:, NC:2 * NC], cols[:, 0:NC], b1p[:, :], rtmp[:, :], K_B1, "b1p_done")

            def b2_masks():
                then_self(absolute(b2a[:, :], b2_bc[:, :]))
                for k, op in enumerate((ALU.is_gt, ALU.is_lt)):
                    last = ve.tensor_scalar(b2m[:, k], b2a[:, :], colsa[:, NC:NC + 1], None, op0=op)
                last.then_inc(q["b2m_done"], 1)

            def perturb_b2():
                v.wait_ge(q["b2rank"], 1)
                tiers(psX[:, 0:P], psX[:, P:2 * P], b2_bc[:, :], b2p_bc[:, :], b2t[:, :], K_B2, "b2p_done")

            def last_parts(b):
                i = b % 2
                v.wait_ge(q["mid_done"], b + 1)
                ve.tensor_tensor(part8[:, i, 2:6:3, :], resid[:, :, :], part8[:, i, 1:5:3, :], op=ALU.subtract).then_inc(q["split_done"], 1)

            for t in range(T_END):
                n = sel_bit(t)
                if t == B1_USE:
                    perturb_b1()
                if t == SEL0:
                    first_cand()
                    dve_mask(0)
                maxima(t, 0)
                b = batch_at(t, AT_NMT)
                if b is not None:
                    v.wait_ge(q["nmhi_done"], b + 1)
                    ve.tensor_tensor(nmT[:, b % 2, 1, :], psX[0:NH, 0:S], nmT[:, b % 2, 0, :], op=ALU.subtract).then_inc(q["nmlo_done"], 1)
                b = batch_at(t, AT_Y)
                if b is not None:
                    v.wait_ge(q["y_done"], b + 1)
                    ve.tensor_tensor(x_all[:, b], x_all[:, b], psX[:, 0:S].rearrange("p (i d) -> p i d", i=NBLK),
                                     op=ALU.add).then_inc(q["x2_done"], 1)
                if t == B2_USE:
                    perturb_b2()
                maxima(t, 1)
                b = batch_at(t, AT_LO)
                if b:
                    last_parts(b)
                if n is not None:
                    v.wait_ge(q["cnt_done"], n + 1)
                    ve.tensor_copy(cnt.rearrange("p a c -> p (a c)"), psX[:, 0:4 * NC]).then_inc(q["cnt_out"], 1)
                maxima(t, 2)
                b, g, e = lagged(t, E_LAG + 1)

                def reciprocals():
                    if b is not None:
                        v.wait_ge(q["ut_done"], e + 1)
                        ve.reciprocal(rden[:, :, :], psU[:, 0:S].rearrange("p (i h r) -> p i h r", i=NBLK, h=HG)[:, :, :, HD]
                                      ).then_inc(q["rd_done"], 1)

                if n is not None:
                    settle(n, reciprocals)
                else:
                    reciprocals()
                if b is not None:
                    v.wait_ge(q["rd_done"], e + 1)
                    if g == 0 and b >= 2:
                        v.wait_ge(q["at_done"], b - 1)
                    pu = psU[:, 0:S].rearrange("p (i h r) -> p i h r", i=NBLK, h=HG)
                    ve.tensor_tensor(A[:, b % 2, :, HG * HD * g:HG * HD * (g + 1)].rearrange("p i (h d) -> p i h d", h=HG),
                                     pu[:, :, :, 0:HD], rden[:, :, :].unsqueeze(3).broadcast_to([P, NBLK, HG, HD]),
                                     op=ALU.mult).then_inc(q["a_done"], 1)
                b = batch_at(t, AT_SPLIT)
                if b is not None:
                    i = b % 2
                    v.wait_ge(q["hi_done"], b + 1)
                    if b >= 2:
                        v.wait_ge(part_w[b % 2], 32 * (b // 2))
                    pq = psQ.rearrange("p (a t) -> p a t", a=2)
                    ve.tensor_tensor(resid[:, :, :], pq, part8[:, i, 0:4:3, :], op=ALU.subtract).then_inc(q["res_done"], 1)
                    v.wait_ge(q["res_done"], b + 1)
                    ve.tensor_copy(part8[:, i, 1:5:3, :], resid[:, :, :]).then_inc(q["mid_done"], 1)
                if t == AT_SPLIT:
                    last_parts(0)
                b = batch_at(t, AT_N1)
                if b is not None:
                    v.wait_ge(q["ln_rstd"], b + 1)
                    if b >= 2:
                        v.wait_ge(q["t_done"], b - 1)
                    for i in range(NBLK):
                        k = 2 * b + i
                        last = ve.tensor_scalar(n1[:, b % 2, i, :], x_all[:, b, i, :], mv1[:, k, 0:1], rs1[:, k:k + 1],
                                                op0=ALU.subtract, op1=ALU.mult)
                    last.then_inc(q["n1_done"], 1)
                b = batch_at(t, AT_T)
                if b is not None and b + 1 < B:
                    ln1(b + 1)
                if t == ROWS_STEP:
                    make_rows()
                if t == VEC_STEP:
                    vector_columns()
                if t == VEC_STEP + 1:
                    router_constants()
                b = t - WO_STEP
                if 0 <= b < B:
                    v.wait_ge(rows_in[b * ROW_DMAS // B], 16)
                    ve.tensor_tensor(woTg[:, b, :], woT[:, :], rows_bc[:, b, 0, :], op=ALU.mult).then_inc(q["wog_done"], 1)
                flat = lambda a: a.rearrange("p c d -> p (c d)")
                if t == W1_STEP:
                    find_tiers(w1a[:, :], cur[:, 2:3], cur[:, 0:1])
                if t == W1_STEP + 1:
                    perturb(w1_sb[:, :], w1p[:, :])
                if t == W2_STEP:
                    find_tiers(w2a[:, :], cur[:, 1:2], cur[:, 3:4])
                if t == W2_STEP + 1:
                    perturb(flat(w2_sb), flat(w2p))
                if t == VEC_STEP:
                    bias_sizes()
                if t == B2_STEP:
                    b2_masks()
                if t == FFN_STEP:
                    router_logits(0)
                for steps, work in ((LN_NEXT_AT, router_stats), (LN_STAT_AT, second_stats), (LN_USE_AT, second_use)):
                    if t in steps:
                        work(steps[t])
            second_stats(NPAIR - 1)
            second_use(NPAIR - 1)
            router_stats(NPAIR - 1)
            router_weights(0)
            for n in range(2 * NPAIR):
                combine(n)
                p = n // 2 + 1
                if p < NPAIR:
                    (router_weights if n % 2 else router_logits)(p)


def slopes():
    start = 2 ** (-2 ** (-(math.log2(NH) - 3)))
    return np.asarray([start * start ** i for i in range(NH)], np.float32)


def bf16_bits(a):
    return (np.ascontiguousarray(a, np.float32).view(np.uint32) >> 16).astype(np.uint16)


def constants():
    rest = slopes()
    sp = []
    for _ in range(3):
        part = (rest.view(np.uint32) & 0xFFFF0000).view(np.float32)
        sp.append(part)
        rest = rest - part
    pos = np.arange(S, dtype=np.float32)
    kc = np.ones((R_BIAS + R_MAX, NH, S), np.float32)
    qc = np.zeros((R_BIAS, NH, S), np.float32)
    for i in range(3):
        kc[i] = sp[i][:, None]
        qc[i] = pos[None, :]
        kc[3 + i] = pos[None, :]
        qc[3 + i] = -sp[i][:, None]
    above = np.where(np.arange(P)[None, :] > np.arange(P)[:, None], NEG, 0.0)
    mask = np.concatenate([above] * HG + [np.eye(P)], axis=1)
    return {"k_const": bf16_bits(kc.reshape(-1, NH * S)), "q_const": bf16_bits(qc.reshape(-1, NH * S)),
            "ident_c": np.eye(P, dtype=np.float32), "mask_c": bf16_bits(mask)}


_INS = [("L0_attn_x", "x"), ("L0_attn_W_qkv", "w_qkv"), ("L0_attn_W_o", "w_o"), ("L0_ffn_W1", "w1"), ("L0_ffn_b1", "b1"),
        ("L0_ffn_W2", "w2"), ("L0_ffn_b2", "b2"), ("L0_ffn_ln_gamma", "gamma"), ("L0_ffn_ln_beta", "beta"),
        ("L0_ffn_Wr", "wr"), ("L0_ffn_br", "br"), ("L0_c", "c"), ("L0_wmod", "wmod")]


def kernel(**inputs):
    import concourse.bacc as bacc
    from concourse.bass_utils import run_bass_kernel_spmd

    nc = bacc.Bacc("TRN2", target_bir_lowering=False, num_devices=1)
    arrays = {f"in_{short}": np.ascontiguousarray(inputs[name]) for name, short in _INS}
    arrays.update({f"in_{name}": a for name, a in constants().items()})
    args = [nc.dram_tensor(n, a.shape, mybir.dt.from_np(a.dtype), kind="ExternalInput").ap() for n, a in arrays.items()]
    parts = nc.dram_tensor("parts", [B, 8, P, S], BF16, kind="Internal").ap()
    rows = nc.dram_tensor("rows_out", [B, 4, D], F32, kind="Internal").ap()
    out = nc.dram_tensor("out_0", [B, S, D], F32, kind="ExternalOutput").ap()
    args = [a.bitcast(BF16) if a.dtype == mybir.dt.uint16 else a for a in args]
    adaln_block(nc, *args, parts, rows, out)
    r = run_bass_kernel_spmd(nc, [arrays], core_ids=[0])
    return r.results[0]["out_0"]
```
